# Optimizing a Trainium2 kernel written in Bass

```python
import numpy as np
import jax
import jax.numpy as jnp

def _softmax(x, axis=-1):
    return jax.nn.softmax(x, axis=axis)

def _gelu(x):
    return jax.nn.gelu(x, approximate=True)

def _silu(x):
    return jax.nn.silu(x)

def _sigmoid(x):
    return jax.nn.sigmoid(x)

def _layernorm(x, axis=-1, eps=1e-05):
    m = jnp.mean(x, axis=axis, keepdims=True)
    v = jnp.var(x, axis=axis, keepdims=True)
    return (x - m) / jnp.sqrt(v + eps)

def _scatter_add(tgt, idx, src, axis=0):
    return tgt.at[idx].add(src)

def _segment_sum(src, seg, n):
    return jax.ops.segment_sum(src, seg, n)
kernel_name = 'mk_recurrent_d1_jaxref_r4_73990b'

def setup_inputs(seed: int=0):
    np.random.seed(seed)
    _w = jnp.asarray

    def _L0_attn_setup():
        import jax, jax.numpy as jnp
        import numpy as np
        HIDDEN = 512
        NUM_HEADS = 16
        HEAD_SIZE = HIDDEN // NUM_HEADS
        SEQ = 512
        BATCH = 2

        def alibi_causal_bias(seq_len: int, num_heads: int) -> jnp.ndarray:
            i = jnp.arange(seq_len)[:, None]
            j = jnp.arange(seq_len)[None, :]
            dist = -(i - j).astype(jnp.float32)
            causal = jnp.where(j > i, -jnp.inf, 0.0)
            base = jnp.where(j > i, 0.0, dist) + causal
            if num_heads <= 8:
                slopes = jnp.asarray([1.0 / 2 ** k for k in range(num_heads)], jnp.float32)
            else:
                slopes = jnp.asarray([1.0 / 2 ** (k / 2) for k in range(num_heads)], jnp.float32)
            return slopes[None, :, None, None] * dist[None, None] * (j <= i)[None, None] + causal[None, None]
        key = jax.random.key(seed)
        ks = jax.random.split(key, 3)
        sd = 1.0 / np.sqrt(HIDDEN)
        return {'x': jax.random.normal(ks[0], (BATCH, SEQ, HIDDEN), jnp.float32), 'Wqkv': jax.random.normal(ks[1], (HIDDEN, 3 * HIDDEN), jnp.float32) * sd, 'bqkv': jnp.zeros((3 * HIDDEN,), jnp.float32), 'Wo': jax.random.normal(ks[2], (HIDDEN, HIDDEN), jnp.float32) * sd, 'bo': jnp.zeros((HIDDEN,), jnp.float32)}
    _L0_attn_in = _L0_attn_setup()

    def _L0_ffn_setup():
        import jax, jax.numpy as jnp
        import numpy as np
        _FP4_LUT = jnp.array([0.0, 0.5, 1.0, 1.5, 2.0, 3.0, 4.0, 6.0, -0.0, -0.5, -1.0, -1.5, -2.0, -3.0, -4.0, -6.0], dtype=jnp.float32)
        GROUP_SIZE = 128
        EPS = 1e-06

        def _dequant_fp4(packed_i32, scales_f16, group_size):
            out_f, in_p = packed_i32.shape
            w = packed_i32.astype(jnp.uint32)
            shifts = jnp.arange(8, dtype=jnp.uint32) * 4
            nib = w[:, :, None] >> shifts & jnp.uint32(15)
            vals = _FP4_LUT[nib.astype(jnp.int32)].reshape(out_f, in_p * 8)
            s = scales_f16.astype(jnp.float32).T
            s_full = jnp.repeat(s, group_size, axis=1)
            return vals * s_full
        key = jax.random.key(seed)
        k1, k2, k3, k4, k5 = jax.random.split(key, 5)
        B, S, H, I = (4, 512, 512, 1408)
        x = jax.random.normal(k1, (B, S, H), dtype=jnp.float32)
        gate_up_packed = jax.random.randint(k2, (2 * I, H // 8), 0, 2147483647, dtype=jnp.int32)
        gate_up_scales = jax.random.uniform(k3, (H // GROUP_SIZE, 2 * I), dtype=jnp.float32).astype(jnp.float16)
        down_packed = jax.random.randint(k4, (H, I // 8), 0, 2147483647, dtype=jnp.int32)
        down_scales = jax.random.uniform(k5, (I // GROUP_SIZE, H), dtype=jnp.float32).astype(jnp.float16)
        return {'x': x, 'gate_up_packed': gate_up_packed, 'gate_up_scales': gate_up_scales, 'down_packed': down_packed, 'down_scales': down_scales}
    _L0_ffn_in = _L0_ffn_setup()
    _d = {'L0_attn_x': _L0_attn_in['x'], 'L0_attn_Wqkv': _L0_attn_in['Wqkv'], 'L0_attn_bqkv': _L0_attn_in['bqkv'], 'L0_attn_Wo': _L0_attn_in['Wo'], 'L0_attn_bo': _L0_attn_in['bo'], 'L0_ffn_gate_up_packed': _L0_ffn_in['gate_up_packed'], 'L0_ffn_gate_up_scales': _L0_ffn_in['gate_up_scales'], 'L0_ffn_down_packed': _L0_ffn_in['down_packed'], 'L0_ffn_down_scales': _L0_ffn_in['down_scales']}
    _x0 = _d['L0_attn_x']
    _d['L0_attn_x'] = jax.random.normal(jax.random.fold_in(jax.random.key(seed), 1), (4, 1024, 512), dtype=_x0.dtype)
    del _x0
    return _d

def reference(L0_attn_x, L0_attn_Wqkv, L0_attn_bqkv, L0_attn_Wo, L0_attn_bo, L0_ffn_gate_up_packed, L0_ffn_gate_up_scales, L0_ffn_down_packed, L0_ffn_down_scales):

    def _L0_attn_ref(x, Wqkv, bqkv, Wo, bo):
        import jax, jax.numpy as jnp
        import numpy as np
        HIDDEN = 512
        NUM_HEADS = 16
        HEAD_SIZE = HIDDEN // NUM_HEADS
        SEQ = 512
        BATCH = 2

        def alibi_causal_bias(seq_len: int, num_heads: int) -> jnp.ndarray:
            i = jnp.arange(seq_len)[:, None]
            j = jnp.arange(seq_len)[None, :]
            dist = -(i - j).astype(jnp.float32)
            causal = jnp.where(j > i, -jnp.inf, 0.0)
            base = jnp.where(j > i, 0.0, dist) + causal
            if num_heads <= 8:
                slopes = jnp.asarray([1.0 / 2 ** k for k in range(num_heads)], jnp.float32)
            else:
                slopes = jnp.asarray([1.0 / 2 ** (k / 2) for k in range(num_heads)], jnp.float32)
            return slopes[None, :, None, None] * dist[None, None] * (j <= i)[None, None] + causal[None, None]
        b, s, h = x.shape
        scale = 1.0 / np.sqrt(HEAD_SIZE)
        qkv = x @ Wqkv + bqkv
        q, k, v = jnp.split(qkv, 3, axis=-1)

        def heads(t):
            return t.reshape(b, s, NUM_HEADS, HEAD_SIZE).transpose(0, 2, 1, 3)
        q, k, v = (heads(q), heads(k), heads(v))
        scores = jnp.einsum('bhid,bhjd->bhij', q, k) * scale
        scores = scores + alibi_causal_bias(s, NUM_HEADS)
        attn = jax.nn.softmax(scores, axis=-1)
        out = jnp.einsum('bhij,bhjd->bhid', attn, v)
        out = out.transpose(0, 2, 1, 3).reshape(b, s, NUM_HEADS * HEAD_SIZE)
        return out @ Wo + bo

    def _L0_ffn_ref(x, gate_up_packed, gate_up_scales, down_packed, down_scales):
        import jax, jax.numpy as jnp
        import numpy as np
        _FP4_LUT = jnp.array([0.0, 0.5, 1.0, 1.5, 2.0, 3.0, 4.0, 6.0, -0.0, -0.5, -1.0, -1.5, -2.0, -3.0, -4.0, -6.0], dtype=jnp.float32)
        GROUP_SIZE = 128
        EPS = 1e-06

        def _dequant_fp4(packed_i32, scales_f16, group_size):
            out_f, in_p = packed_i32.shape
            w = packed_i32.astype(jnp.uint32)
            shifts = jnp.arange(8, dtype=jnp.uint32) * 4
            nib = w[:, :, None] >> shifts & jnp.uint32(15)
            vals = _FP4_LUT[nib.astype(jnp.int32)].reshape(out_f, in_p * 8)
            s = scales_f16.astype(jnp.float32).T
            s_full = jnp.repeat(s, group_size, axis=1)
            return vals * s_full
        I = gate_up_packed.shape[0] // 2
        w_gu = _dequant_fp4(gate_up_packed, gate_up_scales, GROUP_SIZE)
        w_down = _dequant_fp4(down_packed, down_scales, GROUP_SIZE)
        gate_up = jnp.einsum('bsh,oh->bso', x, w_gu)
        gate, up = (gate_up[..., :I], gate_up[..., I:])
        h = jax.nn.silu(gate) * up
        y = jnp.einsum('bsi,hi->bsh', h, w_down)
        rms = jnp.sqrt(jnp.mean(y * y, axis=-1, keepdims=True) + EPS)
        return y / rms
    x = L0_attn_x
    xn = _layernorm(x, axis=-1)
    s = _L0_attn_ref(xn, L0_attn_Wqkv, L0_attn_bqkv, L0_attn_Wo, L0_attn_bo)
    g = _silu(_L0_ffn_ref(xn, L0_ffn_gate_up_packed, L0_ffn_gate_up_scales, L0_ffn_down_packed, L0_ffn_down_scales))
    x = x + s * g
    return x

_drawn_inputs = setup_inputs


def setup_inputs(seed=0):
    import zlib

    import numpy as np

    out = dict(_drawn_inputs(seed))
    spreads = {'L0_attn_bqkv': (0.0, 0.1), 'L0_attn_bo': (0.0, 0.1)}
    factors = {}
    for name, (base, spread) in spreads.items():
        noise = np.random.default_rng([zlib.crc32(name.encode()), seed]).standard_normal(out[name].shape)
        drawn = base * np.exp(spread * noise) if base else spread * noise
        out[name] = jnp.asarray(drawn.astype(out[name].dtype))
    for name, factor in factors.items():
        out[name] = (out[name] * factor).astype(out[name].dtype)
    return out
```

```python
from contextlib import ExitStack

import numpy as np

import concourse.bass as bass
from concourse import mybir

ALU = mybir.AluOpType
ACT = mybir.ActivationFunctionType
AX = mybir.AxisListType
F32 = mybir.dt.float32
F16 = mybir.dt.float16
I32 = mybir.dt.int32
U32 = mybir.dt.uint32

P = 128
HEADS, DH = 16, 32
LN_EPS, RMS_EPS = 1e-5, 1e-6

X_SCALE = 64.0
W_SCALE = 64.0
QK_SCALE = 16.0
V_SCALE = 64.0
P_LOG_SCALE = float(np.log(4096.0))
F_SCALE = 2.0
H_SCALE = 2.0 ** -8
CREDIT = 4


def shape_constants(S):
    slopes = np.array([1.0 / 2 ** (h / 2) for h in range(HEADS)], np.float32)
    tiles = S // P
    a = np.arange(P)[:, None]
    u = np.arange(S)[None, :] - (tiles - 1) * P
    dist = np.where(u > a, -1e30, (u - a) * QK_SCALE * QK_SCALE).astype(np.float32)
    slope = (slopes / (QK_SCALE * QK_SCALE)).astype(np.float32)
    slope = np.ascontiguousarray(np.broadcast_to(np.concatenate([slope, -slope]), (P, 2 * HEADS)))
    per_col = (1.0 / np.sqrt(DH)) / np.repeat(slopes.astype(np.float64), DH)
    qcol = (per_col.reshape(4, P).T * QK_SCALE).astype(np.float32)
    kcol = np.full((P, 4), QK_SCALE, np.float32)
    return {
        "dist": dist,
        "slope": slope,
        "col": np.ascontiguousarray(np.concatenate(
            [qcol / (X_SCALE * W_SCALE), kcol / (X_SCALE * W_SCALE), qcol, kcol], axis=1).astype(np.float32)),
        "ident": np.eye(P, dtype=np.float32),
        "ident16": np.eye(P, dtype=np.float16),
    }


def gated_attention_ffn(nc, x, wqkv, bqkv, wo, bo, gu_packed, gu_scales, dn_packed, dn_scales,
                        dist_t, slope_t, col_t, ident_t, ident16_t, out):
    B, S, D = x.shape
    KT = D // P
    TT = S // P
    F = gu_packed.shape[0] // 2
    FT = F // P
    GU_T = 2 * FT
    GROUPS = HEADS * DH // P
    HPG = P // DH
    HALF = 512
    SUBS = HALF // P

    V_SLOTS = TT // 2
    G_SLOTS = 2 + HPG * TT
    FFN_SLOTS = FT + SUBS
    HALVES = S // HALF
    SB = V_SLOTS + GROUPS * G_SLOTS + HALVES * FFN_SLOTS
    UNITS_OF = [1 if i < 4 else 2 for i in range(TT)]
    UBASE = [sum(UNITS_OF[:i]) for i in range(TT)]
    H_UNITS = sum(UNITS_OF)
    G_UNITS = HPG * H_UNITS
    UB = TT + GROUPS * G_UNITS + TT
    STEPS = HPG * TT
    assert SB % 2 == 0 and UB % 2 == 0 and G_SLOTS % 2 == 0 and G_UNITS % 2 == 0

    with ExitStack() as ctx:
        def sb(name, shape, dt):
            return ctx.enter_context(nc.sbuf_tensor(name, shape, dt))

        def sem(name):
            return ctx.enter_context(nc.semaphore(name))

        wqkv_sb = sb("wqkv_sb", [P, 2, KT, 3 * D], F16)
        wo_sb = sb("wo_sb", [P, 2, KT, D], F16)
        wgu_sb = sb("wgu_sb", [P, 2, KT, 2 * F], F16)
        wdn_sb = sb("wdn_sb", [P, 2, FT, D], F16)
        xT = sb("xT", [P, 2, KT, S], F16)
        vals = sb("vals", [P, TT, HEADS * 2 * DH], F16)
        vals_v = vals[:, :, :].rearrange("p t (h c d) -> p t h c d", h=HEADS, c=2)
        xo = sb("xo", [P, TT, D], F32)
        att = sb("att", [P, 12288], F16)
        sp_buf = att[:, 0:4096].bitcast(F32).rearrange("p (n w) -> p n w", n=2)
        qk_nat = att[:, 4096:8192].rearrange("p (t c s) -> p t c s", t=2, c=2)
        q4 = att[:, 8192:10240].rearrange("p (n s) -> p n s", n=2)
        k4 = att[:, 10240:12288].rearrange("p (n s) -> p n s", n=2)
        hT = att[:, 0:2 * FT * HALF].rearrange("p (c i t) -> p c i t", c=2, i=FT)
        pt_sb = sb("pt_sb", [P, 3, 2, 512], F16)
        dist = sb("dist", [P, S], F32)
        tf = sb("tf", [P, 1024], F32)
        th = sb("th", [P, 2, 512], F32)
        ga = sb("ga", [P, 512], F32)
        xr = sb("xr", [P, 2, D], F32)
        bv = sb("bv", [P, D], F32)
        bo_sb = sb("bo_sb", [P, D], F32)
        oT = sb("oT", [P, 2, KT, P], F16)
        ored = sb("ored", [P, TT, DH], F32)
        ident = sb("ident", [P, P], F32)
        slope = sb("slope", [P, 2 * HEADS], F32)
        slope_v = slope[:, :].rearrange("p (c h) -> p c h", c=2)
        gslope = sb("gslope", [P, 2, HPG], F32)
        col = sb("col", [P, 16], F32)
        colb = sb("colb", [P, 8], F32)
        stats = sb("stats", [P, TT, 6], F32)
        mv = sb("mv", [P, TT, 2], F32)
        base = sb("base", [P, TT], F32)
        rstd = sb("rstd", [P, TT], F32)
        neghalf = sb("neghalf", [P, TT], F32)
        mx = sb("mx", [P, 2], F32)
        nm = sb("nm", [P, 2], F32)
        sums = sb("sums", [P, 2, TT], F32)
        rsum = sb("rsum", [P, TT], F32)
        ssq = sb("ssq", [P, 2], F32)
        rbase = sb("rbase", [P, 2], F32)
        rr = sb("rr", [P, 2], F32)

        slot = [ctx.enter_context(nc.psum_tensor(f"slot{i}", [P, 1024], F32)) for i in range(2)]
        pt = [ctx.enter_context(nc.psum_tensor(f"pt{i}", [P, 512], F32)) for i in range(2)]
        ops = [ctx.enter_context(nc.psum_tensor(f"ops{i}", [P, TT * 2 * DH], F32)) for i in range(2)]

        prepare_weights(nc, wqkv, bqkv, wo, bo, gu_packed, gu_scales, dn_packed, dn_scales,
                        dist_t, slope_t, col_t, ident_t, ident16_t, wqkv_sb, wo_sb, wgu_sb, wdn_sb,
                        xo, vals, xT, att, pt_sb, oT, dist, slope, col, colb, ident, bv, bo_sb, neghalf,
                        slot, pt)

        x_in = sem("x_in")
        bn_done = sem("bn_done")
        mv_done = sem("mv_done")
        base_done = sem("base_done")
        rstd_done = sem("rstd_done")
        xn_done = sem("xn_done")
        slot_full = sem("slot_full")
        slot_free = sem("slot_free")
        unit_full = sem("unit_full")
        unit_hi = sem("unit_hi")
        unit_lo = sem("unit_lo")
        unit_used = sem("unit_used")
        v_hi = sem("v_hi")
        v_lo = sem("v_lo")
        qk_hi = sem("qk_hi")
        qk_lo = sem("qk_lo")
        q4_in = [sem("q4_in0"), sem("q4_in1")]
        gslope_done = sem("gslope_done")
        nm_done = sem("nm_done")
        exp_done = sem("exp_done")
        o_read = sem("o_read")
        rsum_done = sem("rsum_done")
        o_norm = sem("o_norm")
        th_done = sem("th_done")
        ga_done = sem("ga_done")
        h_hi = sem("h_hi")
        h_lo = sem("h_lo")
        ss_done = sem("ss_done")
        rb_done = sem("rb_done")
        rr_done = sem("rr_done")
        xr_in = [sem("xr_in0"), sem("xr_in1")]
        fin = sem("fin")
        out_done = [sem("out_done0"), sem("out_done1")]

        x_t = x.rearrange("b (t p) d -> p (b t) d", p=P)
        x_rows = x.rearrange("b s d -> (b s) d")
        out_rows = out.rearrange("b s d -> (b s) d")

        block = ctx.enter_context(nc.Block())
        C = CREDIT
        held = {e: sem(f"held_{e}") for e in ("act", "dve", "pe")}

        def hold(eng, name, semaphore, value):
            eng.wait_ge(semaphore, value)
            eng.sem_inc(held[name], 1)

        @block.sync
        def _(sp):
            def store(b, n):
                sp.wait_ge(fin, (b * TT + n) * 3 + (3 + C))
                sp.dma_start(out_rows[bass.ds(b * S + n * P, P), :], xr[:, n % 2, :]).then_inc(out_done[n % 2], 16)

            with sp.Fori(0, B) as b:
                sp.wait_ge(unit_full, b * UB + C)
                sp.dma_start(xo[:, :, :], x_t[:, bass.ds(b * TT, TT), :]).then_inc(x_in, 16)
                with sp.Fori(0, GROUPS) as g:
                    hc0 = sp.snap((b * GROUPS + g) * (HPG // 2 * 128))
                    sl0 = sp.snap(b * SB + g * G_SLOTS + V_SLOTS + 2)
                    sp.wait_ge(qk_lo, (b * GROUPS + g) * 2 + (2 + C))
                    for j in range(HPG):
                        if j >= 2:
                            sp.wait_ge(slot_full, sl0 + ((j - 1) * TT + C))
                        rows = slice(DH * j, DH * j + DH)
                        for quarter in range(4):
                            place = slice(DH * quarter, DH * quarter + DH)
                            sp.dma_start(q4[place, j % 2, :], qk_nat[rows, 0, quarter // 2, :]).then_inc(q4_in[j % 2], 16)
                            sp.dma_start(k4[place, j % 2, :], qk_nat[rows, 1, quarter % 2, :]).then_inc(q4_in[j % 2], 16)
                for n in range(TT):
                    sp.wait_ge(out_done[n % 2], b * (TT // 2 * 16) + (n // 2 * 16 + 16 * C))
                    sp.dma_start(xr[:, n % 2, :], x_rows[bass.ds(b * S + n * P, P), :]).then_inc(xr_in[n % 2], 16)
                    if n >= 1:
                        store(b, n - 1)
                store(b, TT - 1)
            for n in range(2):
                sp.wait_ge(out_done[n], B * TT // 2 * 16 + 16 * C)

        @block.gpsimd
        def _(pool):
            for n in range(2):
                pool.sem_inc(out_done[n], 16 * C)
            pool.sem_inc(rstd_done, C)
            pool.sem_inc(rr_done, C)
            with pool.Fori(0, B) as b:
                pool.wait_ge(base_done, b + (1 + C))
                nc.gpsimd.tensor_tensor(rstd[:, :], base[:, :], neghalf[:, :], ALU.pow).then_inc(rstd_done, 1)
                for n in range(TT):
                    pool.wait_ge(rb_done, b * TT + (n + 1 + C))
                    nc.gpsimd.tensor_tensor(rr[:, n % 2:n % 2 + 1], rbase[:, n % 2:n % 2 + 1],
                                            neghalf[:, 0:1], ALU.pow).then_inc(rr_done, 1)

        @block.tensor
        def _(pe):
            for s in (slot_full, unit_full, unit_used):
                pe.sem_inc(s, C)

            def fill_transposes(u0, u, source, blocks):
                pe.wait_ge(unit_lo, u0 + (u - 1 + C))
                for i in range(blocks):
                    mm = nc.tensor.transpose(pt[u % 2][:, i * P:(i + 1) * P], source(i), ident[:, :])
                mm.then_inc(unit_full, 1)

            def three_products(dst, pairs):
                terms = [(l[a], r[c]) for l, r in pairs for a, c in ((0, 0), (0, 1), (1, 0))]
                for i, (l, r) in enumerate(terms):
                    mm = nc.tensor.matmul(dst, l, r, start=(i == 0), stop=(i == len(terms) - 1))
                return mm

            with pe.Fori(0, B) as b:
                sl = pe.snap(b * SB)
                un = pe.snap(b * UB)
                for t in range(TT):
                    pe.wait_ge(xn_done, b * TT + (t + 1 + C))
                    fill_transposes(un, t, lambda i: xo[:, t, i * P:(i + 1) * P], KT)
                pe.wait_ge(unit_lo, un + (TT + C))
                for r in range(V_SLOTS):
                    pe.wait_ge(slot_free, sl + (r - 1 + C))
                    for i in range(2):
                        t = 2 * r + i
                        mm = three_products(slot[r % 2][:, i * 512:(i + 1) * 512], [
                            ([xT[:, c, k, t * P:(t + 1) * P] for c in range(2)],
                             [wqkv_sb[:, c, k, 2 * D:3 * D] for c in range(2)]) for k in range(KT)])
                    mm.then_inc(slot_full, 1)
                hold(pe, "pe", v_lo, b * V_SLOTS + (V_SLOTS + C))

                with pe.Fori(0, GROUPS) as g:
                    gs = pe.snap(b * SB + g * G_SLOTS + V_SLOTS)
                    gu = pe.snap(b * UB + g * G_UNITS + TT)
                    it = pe.snap(b * GROUPS + g)
                    for t in range(2):
                        pe.wait_ge(slot_free, gs + (t - 1 + C))
                        for half in range(S // 512):
                            mm = three_products(slot[t][:, half * 512:(half + 1) * 512], [
                                ([wqkv_sb[:, c, k, bass.ds(g * P + t * D, P)] for c in range(2)],
                                 [xT[:, c, k, half * 512:(half + 1) * 512] for c in range(2)]) for k in range(KT)])
                        mm.then_inc(slot_full, 1)

                    def scores(s):
                        j, i = divmod(s, TT)
                        if i == 0:
                            pe.wait_ge(q4_in[j % 2], it * 256 + (j // 2 + 1) * 128)
                        pe.wait_ge(slot_free, gs + (s + 1 + C))
                        width = (i + 1) * P
                        for c in range(0, width, 512):
                            e = min(c + 512, width)
                            mm = nc.tensor.matmul(slot[s % 2][:, c:e], q4[:, j % 2, i * P:(i + 1) * P],
                                                  k4[:, j % 2, c:e], start=True, stop=True)
                        mm.then_inc(slot_full, 1)

                    def transposes(s):
                        j, i = divmod(s, TT)
                        pe.wait_ge(exp_done, it * STEPS + (s + 1 + C))
                        for n in range(UNITS_OF[i]):
                            u = j * H_UNITS + UBASE[i] + n
                            fill_transposes(gu, u, lambda q: sp_buf[:, s % 2, (4 * n + q) * P:(4 * n + q + 1) * P],
                                            min(4, i + 1 - 4 * n))

                    def times_values(s):
                        j, i = divmod(s, TT)
                        if i == 0:
                            pe.wait_ge(o_read, it * HPG + (j - 1 + C))
                        for n in range(UNITS_OF[i]):
                            u = j * H_UNITS + UBASE[i] + n
                            pe.wait_ge(unit_lo, gu + (u + 1 + C))
                            for q in range(min(4, i + 1 - 4 * n)):
                                t = 4 * n + q
                                for c in range(2):
                                    mm = nc.tensor.matmul(
                                        ops[j % 2][:, i * 64:(i + 1) * 64], pt_sb[:, u % 3, c, q * P:(q + 1) * P],
                                        vals[:, t, bass.ds((g * HPG + j) * 2 * DH, 2 * DH)],
                                        start=(t == 0 and c == 0), stop=(t == i and c == 1))
                            mm.then_inc(unit_used, 1)

                    for s in range(STEPS + 2):
                        if s < STEPS:
                            scores(s)
                        if 1 <= s <= STEPS:
                            transposes(s - 1)
                        if s >= 2:
                            times_values(s - 2)

                for half in range(HALVES):
                    r0 = V_SLOTS + GROUPS * G_SLOTS + half * FFN_SLOTS
                    tok = slice(half * HALF, (half + 1) * HALF)
                    for i in range(FT):
                        r = r0 + i
                        pe.wait_ge(slot_free, sl + (r - 1 + C))
                        for part in range(2):
                            c0 = part * F + i * P
                            mm = three_products(slot[r % 2][:, part * 512:(part + 1) * 512], [
                                ([wgu_sb[:, c, k, c0:c0 + P] for c in range(2)],
                                 [xT[:, c, k, tok] for c in range(2)]) for k in range(KT)])
                        mm.then_inc(slot_full, 1)
                    for q in range(SUBS):
                        n = half * SUBS + q
                        r = r0 + FT + q
                        if n == 0:
                            pe.wait_ge(o_norm, b * HEADS + (HEADS + C))
                        fill_transposes(un, TT + GROUPS * G_UNITS + n, lambda i: xo[:, n, i * P:(i + 1) * P], KT)
                        if q == 0:
                            pe.wait_ge(h_lo, (b * HALVES + half) * FT + (FT + C))
                        pe.wait_ge(slot_free, sl + (r - 1 + C))
                        three_products(slot[r % 2][:, 0:512], [
                            ([hT[:, c, i, q * P:(q + 1) * P] for c in range(2)],
                             [wdn_sb[:, c, i, :] for c in range(2)]) for i in range(FT)])
                        pe.wait_ge(unit_lo, un + (TT + GROUPS * G_UNITS + n + 1 + C))
                        three_products(slot[r % 2][:, 512:1024], [
                            ([oT[:, c, k, :] for c in range(2)],
                             [wo_sb[:, c, k, :] for c in range(2)]) for k in range(KT)]).then_inc(slot_full, 1)

        @block.scalar
        def _(act):
            for s in (unit_hi, v_hi, qk_hi, exp_done, th_done, h_hi, ss_done):
                act.sem_inc(s, C)

            def unit_to_hi(u0, u, dst, width, rows):
                act.wait_ge(unit_full, u0 + (u + 1 + C))
                src = pt[u % 2][:, 0:width]
                if rows:
                    src = src.rearrange("p (k t) -> p k t", k=rows)
                nc.scalar.copy(dst, src).then_inc(unit_hi, 1)

            with act.Fori(0, B) as b:
                un = act.snap(b * UB)
                sl = act.snap(b * SB)
                for t in range(TT):
                    unit_to_hi(un, t, xT[:, 0, :, t * P:(t + 1) * P], KT * P, KT)
                for r in range(V_SLOTS):
                    act.wait_ge(slot_free, sl + (r + 1 + C))
                    nc.scalar.copy(vals_v[:, 2 * r:2 * r + 2, :, 0, :],
                                   tf[:, :].rearrange("p (t h d) -> p t h d", t=2, h=HEADS)).then_inc(v_hi, 1)

                with act.Fori(0, GROUPS) as g:
                    gs = act.snap(b * SB + g * G_SLOTS + V_SLOTS)
                    gu = act.snap(b * UB + g * G_UNITS + TT)
                    it = act.snap(b * GROUPS + g)
                    for t in range(2):
                        hold(act, "act", slot_full, gs + (t + 1 + C))
                        nc.scalar.activation(qk_nat[:, t, 0, :], slot[t][:, :], ACT.Identity,
                                             bias=colb[:, bass.ds(g + 4 * t, 1)],
                                             scale=col[:, bass.ds(g + 4 * t, 1)]).then_inc(qk_hi, 1)
                    for s in range(STEPS + 1):
                        if s < STEPS:
                            j, i = divmod(s, TT)
                            width = (i + 1) * P
                            act.wait_ge(nm_done, it * STEPS + (s + 1 + C))
                            nc.scalar.activation(sp_buf[:, s % 2, 0:width], sp_buf[:, s % 2, 0:width], ACT.Exp,
                                                 bias=nm[:, s % 2:s % 2 + 1],
                                                 scale=gslope[:, 0, j:j + 1],
                                                 accum_out=sums[:, j % 2, i:i + 1]).then_inc(exp_done, 1)
                        if s >= 1:
                            j, i = divmod(s - 1, TT)
                            for n in range(UNITS_OF[i]):
                                u = j * H_UNITS + UBASE[i] + n
                                w = min(4, i + 1 - 4 * n) * P
                                act.wait_ge(unit_used, it * G_UNITS + (u - 2 + C))
                                unit_to_hi(gu, u, pt_sb[:, u % 3, 0, 0:w], w, 0)

                for half in range(HALVES):
                    r0 = V_SLOTS + GROUPS * G_SLOTS + half * FFN_SLOTS
                    for i in range(FT + 1):
                        if i < FT:
                            act.wait_ge(slot_full, sl + (r0 + i + 1 + C))
                            act.wait_ge(slot_free, sl + (r0 + max(i - 1, 0) + C))
                            nc.scalar.activation(th[:, i % 2, :], slot[(r0 + i) % 2][:, 0:512], ACT.Tanh,
                                                 scale=0.5 / (X_SCALE * F_SCALE)).then_inc(th_done, 1)
                        if i >= 1:
                            act.wait_ge(slot_free, sl + (r0 + i + C))
                            nc.scalar.copy(hT[:, 0, i - 1, :], tf[:, (i - 1) % 2 * 512:(i - 1) % 2 * 512 + 512]).then_inc(h_hi, 1)
                    for q in range(SUBS):
                        n = half * SUBS + q
                        r = r0 + FT + q
                        unit_to_hi(un, TT + GROUPS * G_UNITS + n, oT[:, 0, :, :], KT * P, KT)
                        act.wait_ge(slot_full, sl + (r + 1 + C))
                        act.wait_ge(slot_free, sl + (r + C))
                        nc.scalar.activation(th[:, 0, :], slot[r % 2][:, 0:512], ACT.Square,
                                             accum_out=ssq[:, q % 2:q % 2 + 1]).then_inc(ss_done, 1)
                        act.wait_ge(ss_done, b * TT + (n + 1 + C))
                        act.wait_ge(rr_done, b * TT + (n + 1 + C))
                        nc.scalar.activation(th[:, 0, :], slot[r % 2][:, 0:512], ACT.Tanh,
                                             scale=rr[:, n % 2:n % 2 + 1]).then_inc(th_done, 1)

        @block.vector
        def _(dve):
            for s in (bn_done, mv_done, base_done, xn_done, slot_free, unit_lo, v_lo, qk_lo, gslope_done, nm_done,
                      o_read, rsum_done, o_norm, ga_done, h_lo, rb_done, fin):
                dve.sem_inc(s, C)

            def unit_to_lo(u0, u, dst, hi, width, rows):
                dve.wait_ge(unit_hi, u0 + (u + 1 + C))
                src = pt[u % 2][:, 0:width]
                if rows:
                    src = src.rearrange("p (k t) -> p k t", k=rows)
                nc.vector.tensor_tensor(dst, src, hi, ALU.subtract).then_inc(unit_lo, 1)

            with dve.Fori(0, B) as b:
                un = dve.snap(b * UB)
                sl = dve.snap(b * SB)
                bt = dve.snap(b * TT)
                dve.wait_ge(x_in, b * 16 + 16)
                for t in range(TT):
                    nc.vector.bn_stats(stats[:, t, :], xo[:, t, :]).then_inc(bn_done, 1)
                for t in range(TT):
                    hold(dve, "dve", bn_done, bt + (t + 1 + C))
                    nc.vector.bn_aggr(mv[:, t, :], stats[:, t, :]).then_inc(mv_done, 1)
                dve.wait_ge(mv_done, bt + (TT + C))
                nc.vector.tensor_scalar(base[:, :], mv[:, :, 1], X_SCALE ** -2, LN_EPS * X_SCALE ** -2,
                                        ALU.mult, ALU.add).then_inc(base_done, 1)
                dve.wait_ge(rstd_done, b + (1 + C))
                for t in range(TT + 2):
                    if t < TT:
                        nc.vector.tensor_scalar(xo[:, t, :], xo[:, t, :], mv[:, t, 0:1], rstd[:, t:t + 1],
                                                ALU.subtract, ALU.mult).then_inc(xn_done, 1)
                    if t >= 2:
                        q = t - 2
                        unit_to_lo(un, q, xT[:, 1, :, q * P:(q + 1) * P], xT[:, 0, :, q * P:(q + 1) * P], KT * P, KT)

                for r in range(V_SLOTS):
                    dve.wait_ge(slot_full, sl + (r + 1 + C))
                    if r >= 1:
                        dve.wait_ge(v_lo, b * V_SLOTS + (r + C))
                    nc.vector.scalar_tensor_tensor(
                        out=tf[:, :].rearrange("p (t d) -> p t d", t=2),
                        in0=slot[r % 2][:, :].rearrange("p (t d) -> p t d", t=2),
                        scalar=V_SCALE / (X_SCALE * W_SCALE),
                        in1=bv[:, :].unsqueeze(1).broadcast_to([P, 2, D]),
                        op0=ALU.mult, op1=ALU.add).then_inc(slot_free, 1)
                    dve.wait_ge(v_hi, b * V_SLOTS + (r + 1 + C))
                    nc.vector.tensor_tensor(vals_v[:, 2 * r:2 * r + 2, :, 1, :],
                                            tf[:, :].rearrange("p (t h d) -> p t h d", t=2, h=HEADS),
                                            vals_v[:, 2 * r:2 * r + 2, :, 0, :], ALU.subtract).then_inc(v_lo, 1)
                hold(dve, "dve", v_lo, b * V_SLOTS + (V_SLOTS + C))

                with dve.Fori(0, GROUPS) as g:
                    gs = dve.snap(b * SB + g * G_SLOTS + V_SLOTS)
                    gu = dve.snap(b * UB + g * G_UNITS + TT)
                    it = dve.snap(b * GROUPS + g)
                    nc.vector.tensor_copy(gslope[:, :, :], slope_v[:, :, bass.ds(g * HPG, HPG)]).then_inc(gslope_done, 1)
                    for t in range(2):
                        dve.wait_ge(qk_hi, it * 2 + (t + 1 + C))
                        dve.wait_ge(qk_lo, it * 2 + (t + C))
                        nc.vector.tensor_scalar(tf[:, :], slot[t][:, :], col[:, bass.ds(g + 4 * t, 1)],
                                                colb[:, bass.ds(g + 4 * t, 1)], ALU.mult, ALU.add).then_inc(slot_free, 1)
                        dve.wait_ge(slot_free, gs + (t + 1 + C))
                        nc.vector.tensor_tensor(qk_nat[:, t, 1, :], tf[:, :], qk_nat[:, t, 0, :],
                                                ALU.subtract).then_inc(qk_lo, 1)

                    dve.wait_ge(gslope_done, it + (1 + C))

                    def masked_max(s):
                        j, i = divmod(s, TT)
                        width = (i + 1) * P
                        if s >= 2:
                            jj, ii = divmod(s - 2, TT)
                            dve.wait_ge(unit_full, gu + (jj * H_UNITS + UBASE[ii] + UNITS_OF[ii] + C))
                        hold(dve, "dve", slot_full, gs + (s + 3 + C))
                        nc.vector.tensor_tensor_reduce(sp_buf[:, s % 2, 0:width], slot[s % 2][:, 0:width],
                                                       dist[:, S - width:S], 1.0, -3e38, ALU.add, ALU.max,
                                                       mx[:, s % 2:s % 2 + 1]).then_inc(slot_free, 1)
                        dve.wait_ge(slot_free, gs + (s + 3 + C))
                        nc.vector.tensor_scalar(nm[:, s % 2:s % 2 + 1], mx[:, s % 2:s % 2 + 1],
                                                gslope[:, 1, j:j + 1], P_LOG_SCALE,
                                                ALU.mult, ALU.add).then_inc(nm_done, 1)

                    def head_out(j):
                        dve.wait_ge(unit_used, it * G_UNITS + ((j + 1) * H_UNITS + C))
                        dve.wait_ge(o_norm, it * HPG + (j + C))
                        nc.vector.tensor_reduce(ored[:, :, :], ops[j % 2][:, :].rearrange("p (i c d) -> p i d c", i=TT, c=2),
                                                AX.X, ALU.add).then_inc(o_read, 1)
                        nc.vector.reciprocal(rsum[:, :], sums[:, j % 2, :]).then_inc(rsum_done, 1)
                        dve.wait_ge(rsum_done, it * HPG + (j + 1 + C))
                        dve.wait_ge(o_read, it * HPG + (j + 1 + C))
                        nc.vector.tensor_tensor(xo[:, :, bass.ds((g * HPG + j) * DH, DH)], ored[:, :, :],
                                                rsum[:, :].unsqueeze(2).broadcast_to([P, TT, DH]),
                                                ALU.mult).then_inc(o_norm, 1)

                    for s in range(STEPS + 4):
                        if s < STEPS:
                            masked_max(s)
                        if 1 <= s <= STEPS:
                            j, i = divmod(s - 1, TT)
                            for n in range(UNITS_OF[i]):
                                u = j * H_UNITS + UBASE[i] + n
                                w = min(4, i + 1 - 4 * n) * P
                                unit_to_lo(gu, u, pt_sb[:, u % 3, 1, 0:w], pt_sb[:, u % 3, 0, 0:w], w, 0)
                        if s >= TT + 2 and (s - 2) % TT == 0:
                            head_out((s - 2) // TT - 1)

                for half in range(HALVES):
                    r0 = V_SLOTS + GROUPS * G_SLOTS + half * FFN_SLOTS
                    hb = dve.snap((b * HALVES + half) * FT)
                    tb = dve.snap((b * HALVES + half) * (FT + SUBS))
                    for i in range(FT + 1):
                        if i < FT:
                            dve.wait_ge(th_done, tb + (i + 1 + C))
                            dve.wait_ge(slot_free, sl + (r0 + i + C))
                            nc.vector.scalar_tensor_tensor(out=ga[:, :], in0=th[:, i % 2, :], scalar=1.0,
                                                           in1=slot[(r0 + i) % 2][:, 0:512], op0=ALU.add,
                                                           op1=ALU.mult).then_inc(ga_done, 1)
                            dve.wait_ge(ga_done, hb + (i + 1 + C))
                            if i >= 2:
                                dve.wait_ge(h_lo, hb + (i - 1 + C))
                            nc.vector.scalar_tensor_tensor(
                                out=tf[:, i % 2 * 512:i % 2 * 512 + 512], in0=ga[:, :],
                                scalar=0.5 * H_SCALE / (X_SCALE * F_SCALE) ** 2,
                                in1=slot[(r0 + i) % 2][:, 512:1024], op0=ALU.mult, op1=ALU.mult).then_inc(slot_free, 1)
                        if i >= 1:
                            dve.wait_ge(h_hi, hb + (i + C))
                            nc.vector.tensor_tensor(hT[:, 1, i - 1, :], tf[:, (i - 1) % 2 * 512:(i - 1) % 2 * 512 + 512],
                                                    hT[:, 0, i - 1, :], ALU.subtract).then_inc(h_lo, 1)
                    for q in range(SUBS):
                        n = half * SUBS + q
                        r = r0 + FT + q
                        y = slot[r % 2][:, 0:512]
                        unit_to_lo(un, TT + GROUPS * G_UNITS + n, oT[:, 1, :, :], oT[:, 0, :, :], KT * P, KT)
                        dve.wait_ge(ss_done, bt + (n + 1 + C))
                        y_unit = 1.0 / (H_SCALE * F_SCALE)
                        dve_c = (0.5 * y_unit) ** -2
                        nc.vector.tensor_scalar(rbase[:, n % 2:n % 2 + 1], ssq[:, q % 2:q % 2 + 1],
                                                y_unit ** 2 / D * dve_c, RMS_EPS * dve_c,
                                                ALU.mult, ALU.add).then_inc(rb_done, 1)
                        if q == 0:
                            dve.wait_ge(h_lo, hb + (FT + C))
                        dve.wait_ge(fin, bt * 3 + (3 * n + C))
                        nc.vector.scalar_tensor_tensor(out=tf[:, 0:512], in0=slot[r % 2][:, 512:1024],
                                                       scalar=1.0 / (V_SCALE * W_SCALE), in1=bo_sb[:, :],
                                                       op0=ALU.mult, op1=ALU.add).then_inc(fin, 1)
                        dve.wait_ge(th_done, tb + (FT + q + 1 + C))
                        nc.vector.scalar_tensor_tensor(out=ga[:, :], in0=th[:, 0, :], scalar=1.0, in1=y,
                                                       op0=ALU.add, op1=ALU.mult).then_inc(slot_free, 1)
                        dve.wait_ge(slot_free, sl + (r + 1 + C))
                        dve.wait_ge(fin, bt * 3 + (3 * n + 1 + C))
                        nc.vector.scalar_tensor_tensor(out=tf[:, 0:512], in0=ga[:, :], scalar=rr[:, n % 2:n % 2 + 1],
                                                       in1=tf[:, 0:512], op0=ALU.mult, op1=ALU.mult).then_inc(fin, 1)
                        dve.wait_ge(fin, bt * 3 + (3 * n + 2 + C))
                        dve.wait_ge(xr_in[n % 2], b * (TT // 2 * 16) + (n // 2 + 1) * 16)
                        nc.vector.tensor_tensor(xr[:, n % 2, :], tf[:, 0:512], xr[:, n % 2, :],
                                                ALU.add).then_inc(fin, 1)


def prepare_weights(nc, wqkv, bqkv, wo, bo, gu_packed, gu_scales, dn_packed, dn_scales,
                    dist_t, slope_t, col_t, ident_t, ident16_t, wqkv_sb, wo_sb, wgu_sb, wdn_sb,
                    xo, vals, xT, att, pt_sb, oT, dist, slope, col, colb, ident, bv, bo_sb, neghalf,
                    slot, pt):
    D = wo.shape[0]
    KT = D // P
    GU_T = gu_packed.shape[0] // P
    FT = GU_T // 2
    WORDS = D // 8
    DN_T = D // P
    DN_WORDS = dn_packed.shape[1]

    xo_f = xo[:, :, :].rearrange("p t d -> p (t d)")
    wo_in = xo_f[:, 0:KT * D].rearrange("p (k d) -> p k d", k=KT)
    gu_in = xo_f[:, KT * D:KT * D + GU_T * WORDS].bitcast(U32).rearrange("p (t w) -> p t w", t=GU_T)
    vals_f = vals[:, :, :].rearrange("p t n -> p (t n)").bitcast(F32)
    xT_f = xT[:, :, :, :].rearrange("p c k t -> p (c k t)").bitcast(F32)
    wqkv_in = [a[:, n * 3 * D:(n + 1) * 3 * D] for a in (vals_f, xT_f) for n in range(2)]
    att_f = att[:, :].bitcast(F32)
    dn_in = att_f[:, 0:DN_T * DN_WORDS].bitcast(U32).rearrange("p (t w) -> p t w", t=DN_T)
    o = DN_T * DN_WORDS
    mags = att_f[:, o:o + 1024].bitcast(U32).rearrange("p (k w) -> p k w", k=4)
    signs = att_f[:, o + 1024:o + 2048].bitcast(U32).rearrange("p (k w) -> p k w", k=4)
    wf = att_f[:, o + 2048:o + 4096]
    gus_in = pt_sb[:, :, :, :].rearrange("p a b c -> p (a b c)")[0:KT, 0:GU_T * P]
    dns_in = oT[:, :, :, :].rearrange("p a b c -> p (a b c)")[0:FT, 0:D]

    batches = []
    for t0 in range(0, GU_T, 4):
        n = min(4, GU_T - t0)
        batches.append((gu_in[:, t0:t0 + n, :], t0 * KT, n, KT,
                        [[wgu_sb[:, c, g, t0 * P:(t0 + n) * P] for c in range(2)] for g in range(KT)]))
    scale0 = GU_T * KT
    for g0 in range(0, FT, 4):
        ng = min(4, FT - g0)
        batches.append((dn_in[:, :, g0 * 16:(g0 + ng) * 16], scale0, DN_T, ng,
                        [[wdn_sb[:, c, g0 + g, :] for c in range(2)] for g in range(ng)]))
        scale0 += DN_T * ng

    with ExitStack() as ctx:
        def sem(name):
            return ctx.enter_context(nc.semaphore(name))

        scl = ctx.enter_context(nc.sbuf_tensor("scl", [P, scale0], F32))
        ident16 = ctx.enter_context(nc.sbuf_tensor("ident16", [16, 16], F16))
        w_in = [sem(f"w_in{k}") for k in range(KT)]
        wo_loaded = sem("wo_loaded")
        gu_loaded = sem("gu_loaded")
        small_in = sem("small_in")
        split_hi = sem("split_hi")
        split_lo = sem("split_lo")
        scales_t = sem("scales_t")
        bias_done = sem("bias_done")
        scl_done = sem("scl_done")
        bits = sem("bits")
        codes = sem("codes")
        wf_done = sem("wf_done")
        bank_full = sem("bank_full")
        bank_hi = sem("bank_hi")
        bank_lo = sem("bank_lo")
        banks = [slot[0][:, 0:512], slot[0][:, 512:1024], slot[1][:, 0:512], slot[1][:, 512:1024]]

        block = ctx.enter_context(nc.Block())

        @block.sync
        def _(sp):
            sp.dma_start(gu_in, gu_packed.bitcast(U32).rearrange("(t p) w -> p t w", p=P)).then_inc(gu_loaded, 16)
            sp.dma_start(dn_in, dn_packed.bitcast(U32).rearrange("(t p) w -> p t w", p=P)).then_inc(gu_loaded, 16)
            sp.dma_start(gus_in, gu_scales).then_inc(gu_loaded, 16)
            sp.dma_start(dns_in, dn_scales).then_inc(gu_loaded, 16)
            sp.dma_start(ident16[:, :], ident16_t[0:16, 0:16]).then_inc(gu_loaded, 16)
            sp.dma_start(ident[:, :], ident_t).then_inc(gu_loaded, 16)
            for k in range(KT):
                sp.dma_start(wqkv_in[k], wqkv[k * P:(k + 1) * P, :]).then_inc(w_in[k], 16)
            sp.dma_start(wo_in, wo.rearrange("(k p) d -> p k d", p=P)).then_inc(wo_loaded, 16)
            sp.dma_start(dist[:, :], dist_t).then_inc(small_in, 16)
            sp.dma_start(slope[:, :], slope_t).then_inc(small_in, 16)
            sp.dma_start(col[:, :], col_t).then_inc(small_in, 16)
            with nc.allow_non_contiguous_dma(reason="1024 biases, once"):
                sp.dma_start(colb[:, :], bqkv[0:2 * D].rearrange("(t p) -> p t", p=P)).then_inc(small_in, 16)
            sp.dma_start(bv[:, :], bqkv[2 * D:3 * D].partition_broadcast(P)).then_inc(small_in, 16)
            sp.dma_start(bo_sb[:, :], bo.partition_broadcast(P)).then_inc(small_in, 16)
            sp.wait_ge(small_in, 16 * 6)

        @block.tensor
        def _(pe):
            pe.wait_ge(gu_loaded, 16 * 6)
            pg = pt[0][:, :].bitcast(F16)
            for t in range(GU_T):
                nc.tensor.transpose(pg[:, t * KT:(t + 1) * KT], gus_in[:, t * P:(t + 1) * P], ident16[0:KT, 0:KT])
            pd = pt[1][:, :].bitcast(F16)
            for t in range(DN_T):
                mm = nc.tensor.transpose(pd[:, t * 16:t * 16 + FT], dns_in[:, t * P:(t + 1) * P], ident16[0:FT, 0:FT])
            mm.then_inc(scales_t, 1)
            n = 0
            for k, (_, _, no, ng, _) in enumerate(batches):
                pe.wait_ge(wf_done, 4 * (k + 1))
                for g in range(ng):
                    if n >= 4:
                        pe.wait_ge(bank_lo, n - 3)
                    for i in range(no):
                        a = (i * ng + g) * P
                        mm = nc.tensor.transpose(banks[n % 4][:, i * P:(i + 1) * P], wf[:, a:a + P], ident[:, :])
                    mm.then_inc(bank_full, 1)
                    n += 1

        @block.scalar
        def _(act):
            def split(k, source, hi, loaded):
                act.wait_ge(loaded, 16)
                nc.scalar.activation(hi, source, ACT.Copy, scale=W_SCALE).then_inc(split_hi, 1)

            for k in range(KT):
                split(k, wqkv_in[k], wqkv_sb[:, 0, k, :], w_in[k])
            split(KT, wo_in, wo_sb[:, 0, :, :], wo_loaded)
            n = 0
            for _, _, no, ng, dst in batches:
                for g in range(ng):
                    act.wait_ge(bank_full, n + 1)
                    nc.scalar.copy(dst[g][0], banks[n % 4][:, 0:no * P]).then_inc(bank_hi, 1)
                    n += 1

        @block.vector
        def _(dve):
            nc.vector.memset(neghalf[:, :], -0.5)
            unit = F_SCALE * 2.0 ** 14
            dve.wait_ge(scales_t, 1)
            nc.vector.tensor_scalar(scl[:, 0:GU_T * KT], pt[0][:, :].bitcast(F16)[:, 0:GU_T * KT], unit, None,
                                    ALU.mult).then_inc(scl_done, 1)
            pd = pt[1][:, :].bitcast(F16)[:, 0:DN_T * 16].rearrange("p (t g) -> p t g", t=DN_T)
            s0, parts = GU_T * KT, 1
            for g0 in range(0, FT, 4):
                ng = min(4, FT - g0)
                nc.vector.tensor_scalar(scl[:, s0:s0 + DN_T * ng].rearrange("p (t g) -> p t g", t=DN_T),
                                        pd[:, :, g0:g0 + ng], unit, None, ALU.mult).then_inc(scl_done, 1)
                s0 += DN_T * ng
                parts += 1
            dve.wait_ge(scl_done, parts)

            def decode(k):
                words, s0, no, ng, _ = batches[k]
                nw = no * ng * 16
                if k >= 1:
                    dve.wait_ge(wf_done, 4 * k)
                for q in range(4):
                    for dst, bit, mask in ((mags, 9 - 4 * q, 0x0E000E00), (signs, 12 - 4 * q, 0x80008000)):
                        op = ALU.logical_shift_left if bit >= 0 else ALU.logical_shift_right
                        nc.vector.tensor_scalar(dst[:, q, 0:nw].rearrange("p (t w) -> p t w", t=no), words,
                                                abs(bit), mask, op, ALU.bitwise_and).then_inc(bits, 1)
                dve.wait_ge(bits, 8 * (k + 1))
                nc.vector.tensor_tensor(mags[:, :, 0:nw], mags[:, :, 0:nw], signs[:, :, 0:nw],
                                        ALU.bitwise_or).then_inc(codes, 1)
                dve.wait_ge(codes, k + 1)
                blocks = no * ng
                if k >= 1:
                    dve.wait_ge(bank_full, sum(x[3] for x in batches[:k]))
                for q in range(4):
                    nc.vector.tensor_tensor(
                        wf[:, 0:blocks * P].rearrange("p (b w e) -> p b w e", b=blocks, e=8)[:, :, :, q::4],
                        mags[:, q, 0:nw].bitcast(F16).rearrange("p (b w e) -> p b w e", b=blocks, e=2),
                        scl[:, s0:s0 + blocks].unsqueeze(2).unsqueeze(3).broadcast_to([P, blocks, 16, 2]),
                        ALU.mult).then_inc(wf_done, 1)

            def lows(k):
                n = sum(x[3] for x in batches[:k])
                _, _, no, ng, dst = batches[k]
                for g in range(ng):
                    dve.wait_ge(bank_hi, n + 1)
                    nc.vector.tensor_tensor(dst[g][1], banks[n % 4][:, 0:no * P], dst[g][0],
                                            ALU.subtract).then_inc(bank_lo, 1)
                    n += 1

            def split(k, source, hi, lo):
                dve.wait_ge(split_hi, k + 1)
                nc.vector.scalar_tensor_tensor(out=lo, in0=source, scalar=W_SCALE, in1=hi, op0=ALU.mult,
                                               op1=ALU.subtract).then_inc(split_lo, 1)

            for k in range(len(batches)):
                decode(k)
                if k < KT:
                    split(k, wqkv_in[k], wqkv_sb[:, 0, k, :], wqkv_sb[:, 1, k, :])
                if k == KT:
                    split(k, wo_in, wo_sb[:, 0, :, :], wo_sb[:, 1, :, :])
                lows(k)
            dve.wait_ge(small_in, 16 * 6)
            nc.vector.tensor_tensor(colb[:, :], colb[:, :], col[:, 8:16], ALU.mult).then_inc(bias_done, 1)
            nc.vector.tensor_scalar(bv[:, :], bv[:, :], V_SCALE, None, ALU.mult).then_inc(bias_done, 1)
            dve.wait_ge(bias_done, 2)


_INS = ["L0_attn_x", "L0_attn_Wqkv", "L0_attn_bqkv", "L0_attn_Wo", "L0_attn_bo", "L0_ffn_gate_up_packed",
        "L0_ffn_gate_up_scales", "L0_ffn_down_packed", "L0_ffn_down_scales"]


def kernel(**inputs):
    import concourse.bacc as bacc
    from concourse.bass_utils import run_bass_kernel_spmd

    nc = bacc.Bacc("TRN2", target_bir_lowering=False, num_devices=1)
    arrays = {name: np.ascontiguousarray(inputs[name]) for name in _INS}
    arrays |= {f"const_{k}": v for k, v in shape_constants(arrays["L0_attn_x"].shape[1]).items()}
    args = [nc.dram_tensor(f"in_{k}", a.shape, mybir.dt.from_np(a.dtype), kind="ExternalInput").ap()
            for k, a in arrays.items()]
    out = nc.dram_tensor("out_0", arrays["L0_attn_x"].shape, F32, kind="ExternalOutput").ap()
    gated_attention_ffn(nc, *args, out)
    r = run_bass_kernel_spmd(nc, [{f"in_{k}": a for k, a in arrays.items()}], core_ids=[0])
    return r.results[0]["out_0"]
```

```python
from contextlib import ExitStack

import numpy as np

import concourse.bass as bass
from concourse import mybir

ALU = mybir.AluOpType
ACT = mybir.ActivationFunctionType
AX = mybir.AxisListType
F32 = mybir.dt.float32
F16 = mybir.dt.float16
I32 = mybir.dt.int32
U32 = mybir.dt.uint32

P = 128
HEADS, DH = 16, 32
LN_EPS, RMS_EPS = 1e-5, 1e-6

X_SCALE = 64.0
W_SCALE = 64.0
QK_SCALE = 16.0
V_SCALE = 64.0
P_LOG_SCALE = float(np.log(4096.0))
F_SCALE = 2.0
H_SCALE = 2.0 ** -8
CREDIT = 16


def shape_constants(S):
    slopes = np.array([1.0 / 2 ** (h / 2) for h in range(HEADS)], np.float32)
    tiles = S // P
    a = np.arange(P)[:, None]
    u = np.arange(S)[None, :] - (tiles - 1) * P
    dist = np.where(u > a, -1e30, (u - a) * QK_SCALE * QK_SCALE).astype(np.float32)
    slope = (slopes / (QK_SCALE * QK_SCALE)).astype(np.float32)
    slope = np.ascontiguousarray(np.broadcast_to(np.concatenate([slope, -slope]), (P, 2 * HEADS)))
    per_col = (1.0 / np.sqrt(DH)) / np.repeat(slopes.astype(np.float64), DH)
    qcol = (per_col.reshape(4, P).T * QK_SCALE).astype(np.float32)
    kcol = np.full((P, 4), QK_SCALE, np.float32)
    return {
        "dist": dist,
        "slope": slope,
        "col": np.ascontiguousarray(np.concatenate(
            [qcol / (X_SCALE * W_SCALE), kcol / (X_SCALE * W_SCALE), qcol, kcol], axis=1).astype(np.float32)),
        "ident": np.eye(P, dtype=np.float32),
        "ident16": np.eye(P, dtype=np.float16),
    }


def group_schedule(steps, ffn_tiles, subs, first_qk):
    ffn = [("ffn", i, p, 2) for i in range(ffn_tiles) for p in range(2)]
    y = [("y", q, p, 6) for q in range(subs) for p in range(6)]
    qk = [("qk", n, p, 2) for n in range(4) for p in range(2)] if first_qk else []
    weight = [1.0] * steps + [1.7, 1.7]
    per = len(ffn + y + qk) / sum(weight)
    plan, budget, kind = [], 0.0, None
    for s in range(steps + 2):
        budget += weight[s] * per
        plan.append([])
        while (budget >= 0.5 or s == steps + 1) and (ffn or y or qk):
            if kind is None:
                kind = qk if qk and s >= first_qk else ffn or y or qk
            piece = kind.pop(0)
            plan[-1].append(piece)
            budget -= 1.0
            if piece[2] == piece[3] - 1:
                kind = None
                if s < steps + 1 and piece[0] == "ffn" and not ffn:
                    break
    assert not (ffn or y or qk) and all(sum(p[2] == p[3] - 1 for p in now) <= 1 for now in plan)
    return plan


def gated_attention_ffn(nc, x, wqkv, bqkv, wo, bo, gu_packed, gu_scales, dn_packed, dn_scales,
                        dist_t, slope_t, col_t, ident_t, ident16_t, gates, out):
    B, S, D = x.shape
    KT = D // P
    TT = S // P
    F = gu_packed.shape[0] // 2
    FT = F // P
    GROUPS = HEADS * DH // P
    HPG = P // DH
    SUBS = TT // GROUPS
    FW = SUBS * P

    QK_SLOTS = 4
    PRE_SLOTS = QK_SLOTS + TT
    STEPS = HPG * TT
    SB = PRE_SLOTS + GROUPS * STEPS + TT
    TILE = [i for n in range(TT // 2) for i in (n, TT - 1 - n)]
    UNITS_OF = [1 if i < 4 else 2 for i in TILE]
    UBASE = [sum(UNITS_OF[:i]) for i in range(TT)]
    H_UNITS = sum(UNITS_OF)
    G_UNITS = HPG * H_UNITS
    UB = TT + GROUPS * G_UNITS + TT
    WG = FT + SUBS + 4
    WB = GROUPS * WG - 4
    SP_WIDTH = [max(TILE[k::4]) * P + P for k in range(4)]
    SP_AT = [sum(SP_WIDTH[:k]) for k in range(4)]
    SP = sum(SP_WIDTH)
    assert SB % 2 == 0 and UB % 4 == 0 and PRE_SLOTS % 2 == 0 and STEPS % 4 == 0 and G_UNITS % 4 == 0
    PLAN = {more: group_schedule(STEPS, FT, SUBS, 2 * TT + 3 if more else 0) for more in (True, False)}

    def fills(more):
        n, ended = 0, [None]
        for now in PLAN[more]:
            ended.append(None)
            for kind, i, part, parts in now:
                if part == parts - 1:
                    ended[-1] = (n, kind, i)
                    n += 1
        return ended

    ENDED = {more: fills(more) for more in (True, False)}

    def units_before(s):
        return s // TT * H_UNITS + UBASE[s % TT]

    def units_of(s):
        return range(units_before(s), units_before(s + 1))

    with ExitStack() as ctx:
        def sb(name, shape, dt):
            return ctx.enter_context(nc.sbuf_tensor(name, shape, dt))

        def sem(name):
            return ctx.enter_context(nc.semaphore(name))

        wqkv_sb = sb("wqkv_sb", [P, 2, KT, 3 * D], F16)
        wo_sb = sb("wo_sb", [P, 2, KT, D], F16)
        wgu_sb = sb("wgu_sb", [P, 2, KT, 2 * F], F16)
        wdn_sb = sb("wdn_sb", [P, 2, FT, D], F16)
        xT = sb("xT", [P, 2, KT, S], F16)
        vals = sb("vals", [P, TT, HEADS * 2 * DH], F16)
        vals_v = vals[:, :, :].rearrange("p t (h c d) -> p t h c d", h=HEADS, c=2)
        xo = sb("xo", [P, TT, D], F32)
        QN, Q4, K4 = SP, SP + 2 * S, SP + 3 * S
        att = sb("att", [P, SP + 4 * S], F32)
        scores_of = [att[:, SP_AT[k % 4]:SP_AT[k % 4] + (i + 1) * P] for k, i in enumerate(TILE)]
        qk_nat = att[:, QN:Q4].bitcast(F16).rearrange("p (t c s) -> p t c s", t=2, c=2)
        q4 = att[:, Q4:K4].bitcast(F16).rearrange("p (n s) -> p n s", n=2)
        k4 = att[:, K4:K4 + S].bitcast(F16).rearrange("p (n s) -> p n s", n=2)
        x_buf = att[:, 0:TT * D].rearrange("p (t d) -> p t d", t=TT)
        xr = att[:, Q4:K4].rearrange("p (n d) -> p n d", n=2)
        gr = att[:, K4:K4 + S].rearrange("p (n d) -> p n d", n=2)
        hT = sb("hT", [P, 2, FT, FW], F16)
        pt_sb = sb("pt_sb", [P, 4, 2, 512], F16)
        dist = sb("dist", [P, S], F32)
        tf = sb("tf", [P, 512], F32)
        th = sb("th", [P, 512], F32)
        gst = sb("gst", [P, D], F32)
        bo_sb = sb("bo_sb", [P, D], F32)
        ored = sb("ored", [P, TT, DH], F32)
        ident = sb("ident", [P, P], F32)
        slope = sb("slope", [P, 2 * HEADS], F32)
        slope_v = slope[:, :].rearrange("p (c h) -> p c h", c=2)
        gslope = sb("gslope", [P, 2, HPG], F32)
        col = sb("col", [P, 16], F32)
        colb = sb("colb", [P, 8], F32)
        stats = sb("stats", [P, TT, 6], F32)
        mv = sb("mv", [P, TT, 2], F32)
        base = sb("base", [P, TT], F32)
        rstd = sb("rstd", [P, TT], F32)
        neghalf = sb("neghalf", [P, TT], F32)
        mx = sb("mx", [P, 4], F32)
        nm = sb("nm", [P, 4], F32)
        sums = sb("sums", [P, 2, TT], F32)
        rsum = sb("rsum", [P, TT], F32)
        ssq = sb("ssq", [P, SUBS], F32)
        rbase = sb("rbase", [P, SUBS], F32)
        rr = sb("rr", [P, SUBS], F32)

        longs = ctx.enter_context(nc.psum_tensor("longs", [P, 1024], F32))
        shorts = ctx.enter_context(nc.psum_tensor("shorts", [P, 512], F32))
        pt = [ctx.enter_context(nc.psum_tensor(f"pt{i}", [P, 512], F32)) for i in range(2)]
        three = [shorts[:, :], longs[:, 0:512], longs[:, 512:1024]]
        ops = ctx.enter_context(nc.psum_tensor("ops", [P, TT * 2 * DH], F32))
        work = [ctx.enter_context(nc.psum_tensor(f"work{i}", [P, 512], F32)) for i in range(2)]

        prepare_weights(nc, wqkv, bqkv, wo, bo, gu_packed, gu_scales, dn_packed, dn_scales,
                        dist_t, slope_t, col_t, ident_t, ident16_t, wqkv_sb, wo_sb, wgu_sb, wdn_sb,
                        xo, vals, xT, att, hT, pt_sb, dist, slope, col, colb, ident, bo_sb, neghalf,
                        [*three, work[1][:, :]], pt, work[0])

        x_in = sem("x_in")
        bn_done = sem("bn_done")
        mv_done = sem("mv_done")
        base_done = sem("base_done")
        rstd_done = sem("rstd_done")
        xn_done = sem("xn_done")
        slot_full = sem("slot_full")
        slot_free = sem("slot_free")
        unit_full = sem("unit_full")
        unit_hi = sem("unit_hi")
        unit_lo = sem("unit_lo")
        unit_used = sem("unit_used")
        work_full = sem("work_full")
        work_free = sem("work_free")
        v_hi = sem("v_hi")
        qk_hi = sem("qk_hi")
        qk_f32 = sem("qk_f32")
        qk_lo = sem("qk_lo")
        q4_in = [sem("q4_in0"), sem("q4_in1")]
        gslope_done = sem("gslope_done")
        nm_done = sem("nm_done")
        exp_done = sem("exp_done")
        o_read = sem("o_read")
        rsum_done = sem("rsum_done")
        o_norm = sem("o_norm")
        th_done = sem("th_done")
        ga_done = sem("ga_done")
        h_hi = sem("h_hi")
        h_lo = sem("h_lo")
        ss_done = sem("ss_done")
        rb_done = sem("rb_done")
        rr_done = sem("rr_done")
        g_done = sem("g_done")
        g_out = sem("g_out")
        xr_in = [sem("xr_in0"), sem("xr_in1")]
        fin = sem("fin")
        res = sem("res")
        g_free = sem("g_free")
        out_free = sem("out_free")
        out_done = [sem("out_done0"), sem("out_done1")]
        held = {e: sem(f"held_{e}") for e in ("act", "dve", "pe", "sp")}

        x_t = x.rearrange("b (t p) d -> p (b t) d", p=P)
        x_rows = x.rearrange("b s d -> (b s) d")
        out_rows = out.rearrange("b s d -> (b s) d")

        block = ctx.enter_context(nc.Block())
        C = CREDIT

        def hold(eng, name, semaphore, value):
            eng.wait_ge(semaphore, value)
            eng.sem_inc(held[name], 1)

        @block.sync
        def _(sp):
            def load_tokens(b):
                sp.dma_start(x_buf[:, :, :], x_t[:, bass.ds(b * TT, TT), :]).then_inc(x_in, 16)

            def stack_heads(b, g):
                gs = sp.snap(b * SB + g * STEPS + PRE_SLOTS)
                hold(sp, "sp", qk_lo, (b * GROUPS + g) * 4 + (4 + C))
                hold(sp, "sp", out_free, b * TT + C)
                for j in range(HPG):
                    sp.wait_ge(slot_full, gs + ((j - 1) * TT + C))
                    rows = slice(DH * j, DH * j + DH)
                    for quarter in range(4):
                        place = slice(DH * quarter, DH * quarter + DH)
                        sp.dma_start(q4[place, j % 2, :], qk_nat[rows, 0, quarter // 2, :]).then_inc(q4_in[j % 2], 16)
                        sp.dma_start(k4[place, j % 2, :], qk_nat[rows, 1, quarter % 2, :]).then_inc(q4_in[j % 2], 16)

            def row(b, last):
                with sp.Fori(0, GROUPS) as g:
                    stack_heads(b, g)
                hold(sp, "sp", slot_full, b * SB + (PRE_SLOTS + GROUPS * STEPS + C))
                hold(sp, "sp", unit_full, b * UB + (TT + GROUPS * G_UNITS + C))
                if not last:
                    load_tokens(b + 1)
                hold(sp, "sp", g_free, b * TT + (TT + C))
                for n in range(TT):
                    sp.wait_ge(out_free, b * TT + (n - 1 + C))
                    sp.dma_start(xr[:, n % 2, :], x_rows[bass.ds(b * S + n * P, P), :]).then_inc(xr_in[n % 2], 16)
                    sp.dma_start(gr[:, n % 2, :], gates[bass.ds(b * S + n * P, P), :]).then_inc(xr_in[n % 2], 16)

            load_tokens(0)
            with sp.Fori(0, B - 1) as b:
                row(b, False)
            row(B - 1, True)
            sp.wait_ge(g_free, B * TT + C)
            sp.wait_ge(out_free, B * TT + C)

        @block.gpsimd
        def _(pool):
            for s in (h_lo, rstd_done, rr_done, res, g_free, out_free):
                pool.sem_inc(s, C)

            def token_scales(b):
                pool.wait_ge(base_done, b + (1 + C))
                nc.gpsimd.tensor_tensor(rstd[:, :], base[:, :], neghalf[:, :], ALU.pow).then_inc(rstd_done, 1)

            def group(b, g):
                tile0 = pool.snap(b * TT + g * SUBS)
                it = pool.snap(b * GROUPS + g)
                for i in range(FT):
                    pool.wait_ge(h_hi, it * FT + (i + 1 + C))
                    nc.gpsimd.tensor_tensor(hT[:, 1, i, :], th[:, i % 2 * FW:(i % 2 + 1) * FW], hT[:, 0, i, :],
                                            ALU.subtract).then_inc(h_lo, 1)
                for q in range(SUBS):
                    pool.wait_ge(rb_done, tile0 + (q + 1 + C))
                    nc.gpsimd.tensor_tensor(rr[:, q:q + 1], rbase[:, q:q + 1], neghalf[:, 0:1],
                                            ALU.pow).then_inc(rr_done, 1)
                    pool.wait_ge(g_done, tile0 + (q + 1 + C))
                    pool.dma_start(gates[bass.ds(tile0 * P + q * P, P), :], gst[:, :]).then_inc(g_out, 16)
                    pool.wait_ge(g_out, tile0 * 16 + 16 * (q + 1))
                    pool.sem_inc(g_free, 1)

            def stored(b, n):
                pool.wait_ge(out_done[n % 2], b * (TT // 2 * 16) + (n // 2 + 1) * 16)
                pool.sem_inc(out_free, 1)

            def row(b, last):
                with pool.Fori(0, GROUPS) as g:
                    group(b, g)
                for n in range(TT):
                    if n == 4 and not last:
                        token_scales(b + 1)
                    pool.wait_ge(fin, b * 2 * TT + (2 * n + 2 + C))
                    nc.gpsimd.tensor_tensor(xr[:, n % 2, :], gr[:, n % 2, :], xr[:, n % 2, :], ALU.add).then_inc(res, 1)
                    pool.wait_ge(res, b * TT + (n + 1 + C))
                    pool.dma_start(out_rows[bass.ds(b * S + n * P, P), :], xr[:, n % 2, :]).then_inc(out_done[n % 2], 16)
                    if n >= 1:
                        stored(b, n - 1)
                stored(b, TT - 1)

            token_scales(0)
            with pool.Fori(0, B - 1) as b:
                row(b, False)
            row(B - 1, True)

        @block.tensor
        def _(pe):
            for s in (slot_full, unit_full, unit_used, work_full):
                pe.sem_inc(s, C)

            def fill_transposes(u0, u, source, blocks):
                pe.wait_ge(unit_lo, u0 + (u - 1 + C))
                for i in range(blocks):
                    mm = nc.tensor.transpose(pt[u % 2][:, i * P:(i + 1) * P], source(i), ident[:, :])
                mm.then_inc(unit_full, 1)

            def products(dst, pairs, part=0, parts=1):
                terms = [(l[a], r[c]) for l, r in pairs for a, c in ((0, 0), (0, 1), (1, 0))]
                n = len(terms)
                for i in range(part * n // parts, (part + 1) * n // parts):
                    mm = nc.tensor.matmul(dst, *terms[i], start=(i == 0), stop=(i == n - 1))
                return mm

            def qk_pairs(g, t, half):
                return [([wqkv_sb[:, c, k, bass.ds(g * P + t * D, P)] for c in range(2)],
                         [xT[:, c, k, half * 512:(half + 1) * 512] for c in range(2)]) for k in range(KT)]

            def scores(gs, it, s):
                j, i = divmod(s, TT)
                if i == 0:
                    pe.wait_ge(q4_in[j % 2], it * 256 + (j // 2 + 1) * 128)
                pe.wait_ge(slot_free, gs + (s - 1 + C))
                i = TILE[i]
                width = (i + 1) * P
                for c in range(0, width, 512):
                    e = min(c + 512, width)
                    mm = nc.tensor.matmul((shorts, longs)[s % 2][:, c:e], q4[:, j % 2, i * P:(i + 1) * P],
                                          k4[:, j % 2, c:e], start=True, stop=True)
                mm.then_inc(slot_full, 1)

            def group(b, g, more):
                gs = pe.snap(b * SB + g * STEPS + PRE_SLOTS)
                gu = pe.snap(b * UB + g * G_UNITS + TT)
                gw = pe.snap(b * WB + g * WG)
                it = pe.snap(b * GROUPS + g)

                def transposes(s):
                    pe.wait_ge(exp_done, it * STEPS + (s + 1 + C))
                    for n, u in enumerate(units_of(s)):
                        fill_transposes(gu, u, lambda q: scores_of[s % TT][:, (4 * n + q) * P:(4 * n + q + 1) * P],
                                        min(4, TILE[s % TT] + 1 - 4 * n))

                def times_values(s):
                    j, i = divmod(s, TT)
                    if i == 0:
                        pe.wait_ge(o_read, it * HPG + (j + C))
                    i = TILE[i]
                    for n, u in enumerate(units_of(s)):
                        pe.wait_ge(unit_lo, gu + (u + 1 + C))
                        for q in range(min(4, i + 1 - 4 * n)):
                            t = 4 * n + q
                            for c in range(2):
                                mm = nc.tensor.matmul(
                                    ops[:, i * 64:(i + 1) * 64], pt_sb[:, u % 4, c, q * P:(q + 1) * P],
                                    vals[:, t, bass.ds((g * HPG + j) * 2 * DH, 2 * DH)],
                                    start=(t == 0 and c == 0), stop=(t == i and c == 1))
                        mm.then_inc(unit_used, 1)

                def piece(n, kind, i, part, parts):
                    bank = work[n % 2]
                    if part == 0:
                        pe.wait_ge(work_free, gw + (max(n - 1, 0) + C))
                    if kind == "ffn":
                        c0 = part * F + i * P
                        mm = products(bank[:, part * FW:(part + 1) * FW], [
                            ([wgu_sb[:, c, k, c0:c0 + P] for c in range(2)],
                             [xT[:, c, k, bass.ds(g * FW, FW)] for c in range(2)]) for k in range(KT)])
                    elif kind == "y":
                        if part == 0 and i == 0:
                            pe.wait_ge(h_lo, it * FT + (FT + C))
                        mm = products(bank[:, :], [
                            ([hT[:, c, k, i * P:(i + 1) * P] for c in range(2)],
                             [wdn_sb[:, c, k, :] for c in range(2)]) for k in range(FT)], part, parts)
                    else:
                        mm = products(bank[:, :], qk_pairs(g + 1, i // 2, i % 2), part, parts)
                    if part == parts - 1:
                        mm.then_inc(work_full, 1)

                n = 0
                for s in range(STEPS + 2):
                    if 1 <= s <= STEPS:
                        transposes(s - 1)
                    if s >= 2:
                        times_values(s - 2)
                    if s + 2 < STEPS or more and s < STEPS:
                        scores(gs, it, s + 2)
                    for kind, i, part, parts in PLAN[more][s]:
                        piece(n, kind, i, part, parts)
                        n += part == parts - 1

            def prepare(b):
                sl = pe.snap(b * SB)
                un = pe.snap(b * UB)
                for t in range(TT):
                    pe.wait_ge(xn_done, b * TT + (t + 1 + C))
                    fill_transposes(un, t, lambda i: x_buf[:, t, i * P:(i + 1) * P], KT)
                pe.wait_ge(unit_lo, un + (TT + C))
                for r in range(PRE_SLOTS):
                    pe.wait_ge(slot_free, sl + (max(r - 2, 0) + C))
                    if r < QK_SLOTS:
                        mm = products(three[r % 3], qk_pairs(0, r // 2, r % 2))
                    else:
                        t = r - QK_SLOTS
                        mm = products(three[r % 3], [
                            ([xT[:, c, k, t * P:(t + 1) * P] for c in range(2)],
                             [wqkv_sb[:, c, k, 2 * D:3 * D] for c in range(2)]) for k in range(KT)])
                    mm.then_inc(slot_full, 1)

            def row(b, last):
                sl = pe.snap(b * SB)
                un = pe.snap(b * UB)
                for s in range(2):
                    scores(sl + PRE_SLOTS, b * GROUPS, s)
                hold(pe, "pe", slot_free, sl + (PRE_SLOTS + C))
                with pe.Fori(0, GROUPS - 1) as g:
                    group(b, g, True)
                group(b, GROUPS - 1, False)

                def turn_output(n):
                    if n == 0:
                        pe.wait_ge(o_norm, b * HEADS + (HEADS + C))
                    fill_transposes(un, TT + GROUPS * G_UNITS + n, lambda i: xo[:, n, i * P:(i + 1) * P], KT)

                turn_output(0)
                for n in range(TT):
                    if n + 1 < TT:
                        turn_output(n + 1)
                    pe.wait_ge(slot_free, sl + (PRE_SLOTS + GROUPS * STEPS + max(n - 2, 0) + C))
                    pe.wait_ge(unit_lo, un + (TT + GROUPS * G_UNITS + n + 1 + C))
                    products(three[n % 3], [
                        ([pt_sb[:, n % 4, c, k * P:(k + 1) * P] for c in range(2)],
                         [wo_sb[:, c, k, :] for c in range(2)]) for k in range(KT)]).then_inc(slot_full, 1)
                if not last:
                    prepare(b + 1)

            prepare(0)
            with pe.Fori(0, B - 1) as b:
                row(b, False)
            row(B - 1, True)

        @block.scalar
        def _(act):
            for s in (unit_hi, v_hi, qk_f32, qk_hi, exp_done, th_done, h_hi, ss_done):
                act.sem_inc(s, C)

            def unit_to_hi(u0, u, dst, width, rows):
                act.wait_ge(unit_full, u0 + (u + 1 + C))
                src = pt[u % 2][:, 0:width]
                if rows:
                    src = src.rearrange("p (k t) -> p k t", k=rows)
                nc.scalar.copy(dst, src).then_inc(unit_hi, 1)

            def qk_in_f32(it, g, n, src, full, value):
                t = n // 2
                hold(act, "act", full, value)
                hold(act, "act", qk_lo, it * 4 + (n + C))
                nc.scalar.activation(tf[:, :], src, ACT.Identity, bias=colb[:, bass.ds(g + 4 * t, 1)],
                                     scale=col[:, bass.ds(g + 4 * t, 1)]).then_inc(qk_f32, 1)

            def qk_to_hi(it, n):
                act.wait_ge(qk_f32, it * 4 + (n + 1 + C))
                nc.scalar.copy(qk_nat[:, n // 2, 0, n % 2 * 512:(n % 2 + 1) * 512], tf[:, :]).then_inc(qk_hi, 1)

            def group(b, g, more):
                gu = act.snap(b * UB + g * G_UNITS + TT)
                gw = act.snap(b * WB + g * WG)
                it = act.snap(b * GROUPS + g)
                gth = act.snap(it * (FT + SUBS))

                def exponent(s):
                    j, k = divmod(s, TT)
                    if s == 0:
                        act.wait_ge(gslope_done, it + (1 + C))
                    act.wait_ge(nm_done, it * STEPS + (s + 1 + C))
                    nc.scalar.activation(scores_of[k], scores_of[k], ACT.Exp,
                                         bias=nm[:, s % 4:s % 4 + 1], scale=gslope[:, 0, j:j + 1],
                                         accum_out=sums[:, j % 2, TILE[k]:TILE[k] + 1]).then_inc(exp_done, 1)

                def first_read(n, kind, i):
                    bank = work[n % 2]
                    if kind == "ffn":
                        act.wait_ge(work_full, gw + (n + 1 + C))
                        if i < 2:
                            act.wait_ge(g_done, it * SUBS + C)
                        else:
                            act.wait_ge(h_lo, it * FT + (i - 1 + C))
                        nc.scalar.activation(th[:, i % 2 * FW:(i % 2 + 1) * FW], bank[:, 0:FW], ACT.Tanh,
                                             scale=0.5 / (X_SCALE * F_SCALE)).then_inc(th_done, 1)
                    elif kind == "y":
                        act.wait_ge(work_full, gw + (n + 1 + C))
                        if i == 0:
                            act.wait_ge(h_lo, it * FT + (FT + C))
                        else:
                            act.wait_ge(g_done, it * SUBS + (i + C))
                        nc.scalar.activation(th[:, :], bank[:, :], ACT.Square,
                                             accum_out=ssq[:, i:i + 1]).then_inc(ss_done, 1)
                    else:
                        if i == 0:
                            for parity in range(2):
                                hold(act, "act", q4_in[parity], it * 256 + 256)
                        qk_in_f32(it + 1, g + 1, i, bank[:, :], work_full, gw + (n + 1 + C))

                def second_read(n, kind, i):
                    if kind == "ffn":
                        act.wait_ge(work_free, gw + (n + 1 + C))
                        nc.scalar.copy(hT[:, 0, i, :], th[:, i % 2 * FW:(i % 2 + 1) * FW]).then_inc(h_hi, 1)
                    elif kind == "y":
                        act.wait_ge(ss_done, it * SUBS + (i + 1 + C))
                        act.wait_ge(rr_done, it * SUBS + (i + 1 + C))
                        nc.scalar.activation(th[:, :], work[n % 2][:, :], ACT.Tanh,
                                             scale=rr[:, i:i + 1]).then_inc(th_done, 1)
                    else:
                        qk_to_hi(it + 1, i)

                for s in range(STEPS + 3):
                    fill = ENDED[more][s]
                    if fill:
                        first_read(*fill)
                    if 1 <= s <= STEPS:
                        for n, u in enumerate(units_of(s - 1)):
                            w = min(4, TILE[(s - 1) % TT] + 1 - 4 * n) * P
                            act.wait_ge(unit_used, it * G_UNITS + (u - 3 + C))
                            unit_to_hi(gu, u, pt_sb[:, u % 4, 0, 0:w], w, 0)
                    if s < STEPS:
                        exponent(s)
                    if fill:
                        second_read(*fill)

            def prepare(b):
                un = act.snap(b * UB)
                sl = act.snap(b * SB)
                for t in range(TT):
                    unit_to_hi(un, t, xT[:, 0, :, t * P:(t + 1) * P], KT * P, KT)
                act.wait_ge(fin, b * 2 * TT + C)
                for n in range(QK_SLOTS):
                    qk_in_f32(b * GROUPS, 0, n, three[n % 3], slot_full, sl + (n + 1 + C))
                    qk_to_hi(b * GROUPS, n)
                for t in range(TT):
                    r = QK_SLOTS + t
                    act.wait_ge(slot_full, sl + (r + 1 + C))
                    nc.scalar.activation(vals_v[:, t, :, 0, :], three[r % 3].rearrange("p (h d) -> p h d", h=HEADS),
                                         ACT.Copy, scale=V_SCALE / (X_SCALE * W_SCALE)).then_inc(v_hi, 1)

            def row(b, last):
                un = act.snap(b * UB)
                with act.Fori(0, GROUPS - 1) as g:
                    group(b, g, True)
                group(b, GROUPS - 1, False)
                for n in range(TT):
                    unit_to_hi(un, TT + GROUPS * G_UNITS + n, pt_sb[:, n % 4, 0, :], 512, 0)
                if not last:
                    prepare(b + 1)

            prepare(0)
            with act.Fori(0, B - 1) as b:
                row(b, False)
            row(B - 1, True)

        @block.vector
        def _(dve):
            for s in (bn_done, mv_done, base_done, xn_done, slot_free, unit_lo, work_free, qk_lo, gslope_done,
                      nm_done, o_read, rsum_done, o_norm, ga_done, rb_done, g_done, fin):
                dve.sem_inc(s, C)

            def unit_to_lo(u0, u, dst, hi, width, rows):
                dve.wait_ge(unit_hi, u0 + (u + 1 + C))
                src = pt[u % 2][:, 0:width]
                if rows:
                    src = src.rearrange("p (k t) -> p k t", k=rows)
                nc.vector.tensor_tensor(dst, src, hi, ALU.subtract).then_inc(unit_lo, 1)

            def qk_to_lo(it, n):
                t, half = divmod(n, 2)
                cols = slice(half * 512, (half + 1) * 512)
                dve.wait_ge(qk_hi, it * 4 + (n + 1 + C))
                nc.vector.tensor_tensor(qk_nat[:, t, 1, cols], tf[:, :], qk_nat[:, t, 0, cols],
                                        ALU.subtract).then_inc(qk_lo, 1)

            def masked_max(gs, gu, s):
                k = s % TT
                width = (TILE[k] + 1) * P
                dve.wait_ge(unit_full, gu + (units_before(s - 3) + C))
                hold(dve, "dve", slot_full, gs + (s + 1 + C))
                nc.vector.tensor_tensor_reduce(scores_of[k], (shorts, longs)[s % 2][:, 0:width],
                                               dist[:, S - width:S], 1.0, -3e38, ALU.add, ALU.max,
                                               mx[:, s % 4:s % 4 + 1]).then_inc(slot_free, 1)

            def exponent_bias(gs, s, neg_slope):
                dve.wait_ge(slot_free, gs + (s + 1 + C))
                nc.vector.tensor_scalar(nm[:, s % 4:s % 4 + 1], mx[:, s % 4:s % 4 + 1], neg_slope, P_LOG_SCALE,
                                        ALU.mult, ALU.add).then_inc(nm_done, 1)

            def group(b, g, more):
                gs = dve.snap(b * SB + g * STEPS + PRE_SLOTS)
                gu = dve.snap(b * UB + g * G_UNITS + TT)
                gw = dve.snap(b * WB + g * WG)
                it = dve.snap(b * GROUPS + g)
                gth = dve.snap(it * (FT + SUBS))
                dve.wait_ge(exp_done, it * STEPS + C)
                dve.wait_ge(nm_done, it * STEPS + (1 + C))
                nc.vector.tensor_copy(gslope[:, :, :], slope_v[:, :, bass.ds(g * HPG, HPG)]).then_inc(gslope_done, 1)
                dve.wait_ge(gslope_done, it + (1 + C))

                def head_out(j):
                    dve.wait_ge(unit_used, it * G_UNITS + ((j + 1) * H_UNITS + C))
                    dve.wait_ge(o_norm, it * HPG + (j + C))
                    nc.vector.tensor_reduce(ored[:, :, :], ops[:, :].rearrange("p (i c d) -> p i d c", i=TT, c=2),
                                            AX.X, ALU.add).then_inc(o_read, 1)
                    nc.vector.reciprocal(rsum[:, :], sums[:, j % 2, :]).then_inc(rsum_done, 1)
                    dve.wait_ge(rsum_done, it * HPG + (j + 1 + C))
                    dve.wait_ge(o_read, it * HPG + (j + 1 + C))
                    nc.vector.tensor_tensor(xo[:, :, bass.ds((g * HPG + j) * DH, DH)], ored[:, :, :],
                                            rsum[:, :].unsqueeze(2).broadcast_to([P, TT, DH]),
                                            ALU.mult).then_inc(o_norm, 1)

                def first_read(n, kind, i):
                    half = th[:, i % 2 * FW:(i % 2 + 1) * FW]
                    if kind == "ffn":
                        dve.wait_ge(th_done, gth + (i + 1 + C))
                        nc.vector.scalar_tensor_tensor(out=half, in0=half, scalar=1.0, in1=work[n % 2][:, 0:FW],
                                                       op0=ALU.add, op1=ALU.mult).then_inc(ga_done, 1)
                    elif kind == "y":
                        dve.wait_ge(ss_done, it * SUBS + (i + 1 + C))
                        y_unit = 1.0 / (H_SCALE * F_SCALE)
                        c = (0.5 * y_unit) ** -2
                        nc.vector.tensor_scalar(rbase[:, i:i + 1], ssq[:, i:i + 1], y_unit ** 2 / D * c,
                                                RMS_EPS * c, ALU.mult, ALU.add).then_inc(rb_done, 1)
                    else:
                        dve.wait_ge(qk_f32, it * 4 + (i + 5 + C))
                        dve.sem_inc(work_free, 1)

                def second_read(n, kind, i):
                    if kind == "ffn":
                        half = th[:, i % 2 * FW:(i % 2 + 1) * FW]
                        dve.wait_ge(ga_done, it * FT + (i + 1 + C))
                        nc.vector.scalar_tensor_tensor(
                            out=half, in0=half, scalar=0.5 * H_SCALE / (X_SCALE * F_SCALE) ** 2,
                            in1=work[n % 2][:, FW:2 * FW], op0=ALU.mult, op1=ALU.mult).then_inc(work_free, 1)

                def last_read(n, kind, i):
                    if kind == "y":
                        dve.wait_ge(th_done, gth + (FT + i + 1 + C))
                        nc.vector.scalar_tensor_tensor(out=th[:, :], in0=th[:, :], scalar=1.0, in1=work[n % 2][:, :],
                                                       op0=ALU.add, op1=ALU.mult).then_inc(work_free, 1)
                        dve.wait_ge(work_free, gw + (n + 1 + C))
                        dve.wait_ge(g_free, it * SUBS + (i + C))
                        nc.vector.tensor_scalar(gst[:, :], th[:, :], rr[:, i:i + 1], None,
                                                ALU.mult).then_inc(g_done, 1)
                    elif kind == "qk":
                        qk_to_lo(it + 1, i)

                for s in range(STEPS + 3):
                    fill = ENDED[more][s]
                    ahead = s + 1 < STEPS + more
                    if ahead:
                        masked_max(gs, gu, s + 1)
                    if fill:
                        first_read(*fill)
                    if ahead:
                        j = (s + 1) // TT
                        exponent_bias(gs, s + 1, gslope[:, 1, j:j + 1] if j < HPG else
                                      slope_v[:, 1, bass.ds(g * HPG + HPG, 1)])
                    if fill:
                        second_read(*fill)
                    if 1 <= s <= STEPS:
                        for n, u in enumerate(units_of(s - 1)):
                            w = min(4, TILE[(s - 1) % TT] + 1 - 4 * n) * P
                            unit_to_lo(gu, u, pt_sb[:, u % 4, 1, 0:w], pt_sb[:, u % 4, 0, 0:w], w, 0)
                    if fill:
                        last_read(*fill)
                    if s > TT and (s - 1) % TT == 0:
                        head_out((s - 1) // TT - 1)

            def token_stats(b, t):
                nc.vector.bn_stats(stats[:, t, :], x_buf[:, t, :]).then_inc(bn_done, 1)

            def token_base(b):
                bt = dve.snap(b * TT)
                for t in range(TT):
                    hold(dve, "dve", bn_done, bt + (t + 1 + C))
                    nc.vector.bn_aggr(mv[:, t, :], stats[:, t, :]).then_inc(mv_done, 1)
                dve.wait_ge(mv_done, bt + (TT + C))
                nc.vector.tensor_scalar(base[:, :], mv[:, :, 1], X_SCALE ** -2, LN_EPS * X_SCALE ** -2,
                                        ALU.mult, ALU.add).then_inc(base_done, 1)

            def normalise(b, t):
                if t == 0:
                    dve.wait_ge(rstd_done, b + (1 + C))
                nc.vector.tensor_scalar(x_buf[:, t, :], x_buf[:, t, :], mv[:, t, 0:1], rstd[:, t:t + 1],
                                        ALU.subtract, ALU.mult).then_inc(xn_done, 1)

            def prepare(b):
                un = dve.snap(b * UB)
                sl = dve.snap(b * SB)
                for t in range(TT):
                    unit_to_lo(un, t, xT[:, 1, :, t * P:(t + 1) * P], xT[:, 0, :, t * P:(t + 1) * P], KT * P, KT)
                for n in range(QK_SLOTS):
                    dve.wait_ge(qk_f32, b * GROUPS * 4 + (n + 1 + C))
                    dve.sem_inc(slot_free, 1)
                    qk_to_lo(b * GROUPS, n)
                for t in range(TT):
                    r = QK_SLOTS + t
                    dve.wait_ge(v_hi, b * TT + (t + 1 + C))
                    nc.vector.scalar_tensor_tensor(
                        out=vals_v[:, t, :, 1, :], in0=three[r % 3].rearrange("p (h d) -> p h d", h=HEADS),
                        scalar=V_SCALE / (X_SCALE * W_SCALE), in1=vals_v[:, t, :, 0, :],
                        op0=ALU.mult, op1=ALU.subtract).then_inc(slot_free, 1)
                masked_max(sl + PRE_SLOTS, un + TT, 0)
                exponent_bias(sl + PRE_SLOTS, 0, slope_v[:, 1, 0:1])

            def row(b, last):
                un = dve.snap(b * UB)
                sl = dve.snap(b * SB)
                bt = dve.snap(b * TT)
                with dve.Fori(0, GROUPS - 1) as g:
                    group(b, g, True)
                group(b, GROUPS - 1, False)

                def combine(m):
                    dve.wait_ge(slot_full, sl + (PRE_SLOTS + GROUPS * STEPS + m + 1 + C))
                    dve.wait_ge(fin, bt * 2 + (2 * m + C))
                    nc.vector.scalar_tensor_tensor(out=tf[:, :], in0=three[m % 3],
                                                   scalar=1.0 / (V_SCALE * W_SCALE), in1=bo_sb[:, :],
                                                   op0=ALU.mult, op1=ALU.add).then_inc(fin, 1)
                    dve.wait_ge(fin, bt * 2 + (2 * m + 1 + C))
                    dve.sem_inc(slot_free, 1)
                    dve.wait_ge(xr_in[m % 2], b * (TT // 2 * 32) + (m // 2 + 1) * 32)
                    nc.vector.tensor_tensor(gr[:, m % 2, :], tf[:, :], gr[:, m % 2, :], ALU.mult).then_inc(fin, 1)

                for n in range(TT):
                    unit_to_lo(un, TT + GROUPS * G_UNITS + n, pt_sb[:, n % 4, 1, :], pt_sb[:, n % 4, 0, :], 512, 0)
                    if not last:
                        if n == 0:
                            dve.wait_ge(x_in, b * 16 + 32)
                        if n < TT // 2:
                            for t in (2 * n, 2 * n + 1):
                                token_stats(b + 1, t)
                        if n == TT // 2:
                            token_base(b + 1)
                    if n >= 1:
                        combine(n - 1)
                    if not last and n > TT // 2:
                        for t in range((n - 5) * TT // 3, (n - 4) * TT // 3):
                            normalise(b + 1, t)
                combine(TT - 1)
                if not last:
                    prepare(b + 1)

            dve.wait_ge(x_in, 16)
            for t in range(TT):
                token_stats(0, t)
            token_base(0)
            for t in range(TT):
                normalise(0, t)
            prepare(0)
            with dve.Fori(0, B - 1) as b:
                row(b, False)
            row(B - 1, True)


def prepare_weights(nc, wqkv, bqkv, wo, bo, gu_packed, gu_scales, dn_packed, dn_scales,
                    dist_t, slope_t, col_t, ident_t, ident16_t, wqkv_sb, wo_sb, wgu_sb, wdn_sb,
                    xo, vals, xT, att, hT, pt_sb, dist, slope, col, colb, ident, bo_sb, neghalf,
                    banks, pt, work):
    D = wo.shape[0]
    KT = D // P
    GU_T = gu_packed.shape[0] // P
    FT = GU_T // 2
    WORDS = D // 8
    DN_T = D // P
    DN_WORDS = dn_packed.shape[1]

    xo_f = xo[:, :, :].rearrange("p t d -> p (t d)")
    wo_in = xo_f[:, 0:KT * D].rearrange("p (k d) -> p k d", k=KT)
    gu_in = xo_f[:, KT * D:KT * D + GU_T * WORDS].bitcast(U32).rearrange("p (t w) -> p t w", t=GU_T)
    vals_f = vals[:, :, :].rearrange("p t n -> p (t n)").bitcast(F32)
    xT_f = xT[:, :, :, :].rearrange("p c k t -> p (c k t)").bitcast(F32)
    wqkv_in = [a[:, n * 3 * D:(n + 1) * 3 * D] for a in (vals_f, xT_f) for n in range(2)]
    att_f = att[:, :]
    dn_in = att_f[:, 0:DN_T * DN_WORDS].bitcast(U32).rearrange("p (t w) -> p t w", t=DN_T)
    o = DN_T * DN_WORDS
    mags = att_f[:, o:o + 1024].bitcast(U32).rearrange("p (k w) -> p k w", k=4)
    signs = att_f[:, o + 1024:o + 2048].bitcast(U32).rearrange("p (k w) -> p k w", k=4)
    wf = att_f[:, o + 2048:o + 4096]
    gus_in = pt_sb[:, :, :, :].rearrange("p a b c -> p (a b c)")[0:KT, 0:GU_T * P]

    batches = []
    for t0 in range(0, GU_T, 4):
        n = min(4, GU_T - t0)
        batches.append((gu_in[:, t0:t0 + n, :], t0 * KT, n, KT,
                        [[wgu_sb[:, c, g, t0 * P:(t0 + n) * P] for c in range(2)] for g in range(KT)]))
    scale0 = GU_T * KT
    for g0 in range(0, FT, 4):
        ng = min(4, FT - g0)
        batches.append((dn_in[:, :, g0 * 16:(g0 + ng) * 16], scale0, DN_T, ng,
                        [[wdn_sb[:, c, g0 + g, :] for c in range(2)] for g in range(ng)]))
        scale0 += DN_T * ng

    with ExitStack() as ctx:
        def sem(name):
            return ctx.enter_context(nc.semaphore(name))

        hT_f = hT[:, :, :, :].rearrange("p c k t -> p (c k t)")
        scl = hT_f[:, 0:2 * scale0].bitcast(F32)
        dns = hT_f[:, 2 * scale0:2 * scale0 + D]
        dns_in = dns[0:FT, :]
        bv_in = att_f[:, o + 4096:o + 4096 + KT]
        bv_rows = att_f[:, o + 4112:o + 4112 + KT * P].bitcast(F16).rearrange("p (c k m) -> p c k m", c=2, k=KT)
        ident16 = hT_f[0:16, 2 * scale0 + D:2 * scale0 + D + 16]
        w_in = [sem(f"w_in{k}") for k in range(KT)]
        wo_loaded = sem("wo_loaded")
        gu_loaded = sem("gu_loaded")
        small_in = sem("small_in")
        split_hi = sem("split_hi")
        split_lo = sem("split_lo")
        scales_t = sem("scales_t")
        bias_done = sem("bias_done")
        bv_done = sem("bv_done")
        bv_wo = sem("bv_wo")
        scl_done = sem("scl_done")
        bits = sem("bits")
        codes = sem("codes")
        wf_done = sem("wf_done")
        bank_full = sem("bank_full")
        bank_hi = sem("bank_hi")
        bank_lo = sem("bank_lo")

        block = ctx.enter_context(nc.Block())

        @block.sync
        def _(sp):
            sp.dma_start(gu_in, gu_packed.bitcast(U32).rearrange("(t p) w -> p t w", p=P)).then_inc(gu_loaded, 16)
            sp.dma_start(dn_in, dn_packed.bitcast(U32).rearrange("(t p) w -> p t w", p=P)).then_inc(gu_loaded, 16)
            sp.dma_start(gus_in, gu_scales).then_inc(gu_loaded, 16)
            sp.dma_start(dns_in, dn_scales).then_inc(gu_loaded, 16)
            sp.dma_start(ident16[:, :], ident16_t[0:16, 0:16]).then_inc(gu_loaded, 16)
            sp.dma_start(ident[:, :], ident_t).then_inc(gu_loaded, 16)
            for k in range(KT):
                sp.dma_start(wqkv_in[k], wqkv[k * P:(k + 1) * P, :]).then_inc(w_in[k], 16)
            sp.dma_start(wo_in, wo.rearrange("(k p) d -> p k d", p=P)).then_inc(wo_loaded, 16)
            sp.dma_start(dist[:, :], dist_t).then_inc(small_in, 16)
            sp.dma_start(slope[:, :], slope_t).then_inc(small_in, 16)
            sp.dma_start(col[:, :], col_t).then_inc(small_in, 16)
            with nc.allow_non_contiguous_dma(reason="1024 biases, once"):
                sp.dma_start(colb[:, :], bqkv[0:2 * D].rearrange("(t p) -> p t", p=P)).then_inc(small_in, 16)
                sp.dma_start(bv_in, bqkv[2 * D:3 * D].rearrange("(t p) -> p t", p=P)).then_inc(small_in, 16)
            sp.dma_start(bo_sb[:, :], bo.partition_broadcast(P)).then_inc(small_in, 16)
            sp.wait_ge(small_in, 16 * 6)

        @block.tensor
        def _(pe):
            pe.wait_ge(gu_loaded, 16 * 6)
            pg = pt[0][:, :].bitcast(F16)
            for t in range(GU_T):
                nc.tensor.transpose(pg[:, t * KT:(t + 1) * KT], gus_in[:, t * P:(t + 1) * P], ident16[0:KT, 0:KT])
            pd = pt[1][:, :].bitcast(F16)
            for t in range(DN_T):
                mm = nc.tensor.transpose(pd[:, t * 16:t * 16 + FT], dns_in[:, t * P:(t + 1) * P], ident16[0:FT, 0:FT])
            mm.then_inc(scales_t, 1)
            pe.wait_ge(bv_done, 2)
            terms = [(bv_rows[:, a, k, :], wo_sb[:, c, k, :]) for k in range(KT) for a, c in ((0, 0), (0, 1), (1, 0))]
            for i, (l, r) in enumerate(terms):
                mm = nc.tensor.matmul(work[:, :], l, r, start=(i == 0), stop=(i == len(terms) - 1))
            mm.then_inc(bv_wo, 1)
            n = 0
            for k, (_, _, no, ng, _) in enumerate(batches):
                pe.wait_ge(wf_done, 4 * (k + 1))
                for g in range(ng):
                    if n >= 4:
                        pe.wait_ge(bank_lo, n - 3)
                    for i in range(no):
                        a = (i * ng + g) * P
                        mm = nc.tensor.transpose(banks[n % 4][:, i * P:(i + 1) * P], wf[:, a:a + P], ident[:, :])
                    mm.then_inc(bank_full, 1)
                    n += 1

        @block.scalar
        def _(act):
            def split(source, hi, loaded):
                act.wait_ge(loaded, 16)
                nc.scalar.activation(hi, source, ACT.Copy, scale=W_SCALE).then_inc(split_hi, 1)

            split(wo_in, wo_sb[:, 0, :, :], wo_loaded)
            for k in range(KT):
                split(wqkv_in[k], wqkv_sb[:, 0, k, :], w_in[k])
            n = 0
            for _, _, no, ng, dst in batches:
                for g in range(ng):
                    act.wait_ge(bank_full, n + 1)
                    nc.scalar.copy(dst[g][0], banks[n % 4][:, 0:no * P]).then_inc(bank_hi, 1)
                    n += 1

        @block.vector
        def _(dve):
            nc.vector.memset(neghalf[:, :], -0.5)
            unit = F_SCALE * 2.0 ** 14
            dve.wait_ge(scales_t, 1)
            nc.vector.tensor_scalar(scl[:, 0:GU_T * KT], pt[0][:, :].bitcast(F16)[:, 0:GU_T * KT], unit, None,
                                    ALU.mult).then_inc(scl_done, 1)
            pd = pt[1][:, :].bitcast(F16)[:, 0:DN_T * 16].rearrange("p (t g) -> p t g", t=DN_T)
            s0, parts = GU_T * KT, 1
            for g0 in range(0, FT, 4):
                ng = min(4, FT - g0)
                nc.vector.tensor_scalar(scl[:, s0:s0 + DN_T * ng].rearrange("p (t g) -> p t g", t=DN_T),
                                        pd[:, :, g0:g0 + ng], unit, None, ALU.mult).then_inc(scl_done, 1)
                s0 += DN_T * ng
                parts += 1
            dve.wait_ge(scl_done, parts)

            def decode(k):
                words, s0, no, ng, _ = batches[k]
                nw = no * ng * 16
                if k >= 1:
                    dve.wait_ge(wf_done, 4 * k)
                for q in range(4):
                    for dst, bit, mask in ((mags, 9 - 4 * q, 0x0E000E00), (signs, 12 - 4 * q, 0x80008000)):
                        op = ALU.logical_shift_left if bit >= 0 else ALU.logical_shift_right
                        nc.vector.tensor_scalar(dst[:, q, 0:nw].rearrange("p (t w) -> p t w", t=no), words,
                                                abs(bit), mask, op, ALU.bitwise_and).then_inc(bits, 1)
                dve.wait_ge(bits, 8 * (k + 1))
                nc.vector.tensor_tensor(mags[:, :, 0:nw], mags[:, :, 0:nw], signs[:, :, 0:nw],
                                        ALU.bitwise_or).then_inc(codes, 1)
                dve.wait_ge(codes, k + 1)
                blocks = no * ng
                if k >= 1:
                    dve.wait_ge(bank_full, sum(x[3] for x in batches[:k]))
                for q in range(4):
                    nc.vector.tensor_tensor(
                        wf[:, 0:blocks * P].rearrange("p (b w e) -> p b w e", b=blocks, e=8)[:, :, :, q::4],
                        mags[:, q, 0:nw].bitcast(F16).rearrange("p (b w e) -> p b w e", b=blocks, e=2),
                        scl[:, s0:s0 + blocks].unsqueeze(2).unsqueeze(3).broadcast_to([P, blocks, 16, 2]),
                        ALU.mult).then_inc(wf_done, 1)

            def lows(k):
                n = sum(x[3] for x in batches[:k])
                _, _, no, ng, dst = batches[k]
                for g in range(ng):
                    dve.wait_ge(bank_hi, n + 1)
                    nc.vector.tensor_tensor(dst[g][1], banks[n % 4][:, 0:no * P], dst[g][0],
                                            ALU.subtract).then_inc(bank_lo, 1)
                    n += 1

            def split(k, source, hi, lo):
                dve.wait_ge(split_hi, k + 1)
                nc.vector.scalar_tensor_tensor(out=lo, in0=source, scalar=W_SCALE, in1=hi, op0=ALU.mult,
                                               op1=ALU.subtract).then_inc(split_lo, 1)

            split(0, wo_in, wo_sb[:, 0, :, :], wo_sb[:, 1, :, :])
            dve.wait_ge(small_in, 16 * 6)
            rows = bv_in.unsqueeze(2).broadcast_to([P, KT, P])
            nc.vector.tensor_scalar(bv_rows[:, 0, :, :], rows, V_SCALE, None, ALU.mult).then_inc(bv_done, 1)
            dve.wait_ge(bv_done, 1)
            nc.vector.scalar_tensor_tensor(out=bv_rows[:, 1, :, :], in0=rows, scalar=V_SCALE, in1=bv_rows[:, 0, :, :],
                                           op0=ALU.mult, op1=ALU.subtract).then_inc(bv_done, 1)
            for k in range(len(batches)):
                decode(k)
                if k < KT:
                    split(k + 1, wqkv_in[k], wqkv_sb[:, 0, k, :], wqkv_sb[:, 1, k, :])
                lows(k)
            nc.vector.tensor_tensor(colb[:, :], colb[:, :], col[:, 8:16], ALU.mult).then_inc(bias_done, 1)
            dve.wait_ge(bv_wo, 1)
            nc.vector.scalar_tensor_tensor(out=bo_sb[:, :], in0=work[:, :], scalar=1.0 / (V_SCALE * W_SCALE),
                                           in1=bo_sb[:, :], op0=ALU.mult, op1=ALU.add).then_inc(bias_done, 1)
            dve.wait_ge(bias_done, 2)


_INS = ["L0_attn_x", "L0_attn_Wqkv", "L0_attn_bqkv", "L0_attn_Wo", "L0_attn_bo", "L0_ffn_gate_up_packed",
        "L0_ffn_gate_up_scales", "L0_ffn_down_packed", "L0_ffn_down_scales"]


def kernel(**inputs):
    import concourse.bacc as bacc
    from concourse.bass_utils import run_bass_kernel_spmd

    nc = bacc.Bacc("TRN2", target_bir_lowering=False, num_devices=1)
    arrays = {name: np.ascontiguousarray(inputs[name]) for name in _INS}
    arrays |= {f"const_{k}": v for k, v in shape_constants(arrays["L0_attn_x"].shape[1]).items()}
    args = [nc.dram_tensor(f"in_{k}", a.shape, mybir.dt.from_np(a.dtype), kind="ExternalInput").ap()
            for k, a in arrays.items()]
    out = nc.dram_tensor("out_0", arrays["L0_attn_x"].shape, F32, kind="ExternalOutput").ap()
    gates = nc.dram_tensor("gates", [out.shape[0] * out.shape[1], out.shape[2]], F32, kind="Internal").ap()
    gated_attention_ffn(nc, *args, gates, out)
    r = run_bass_kernel_spmd(nc, [{f"in_{k}": a for k, a in arrays.items()}], core_ids=[0])
    return r.results[0]["out_0"]
```

```python
from contextlib import ExitStack

import numpy as np

import concourse.bass as bass
from concourse import mybir

ALU = mybir.AluOpType
ACT = mybir.ActivationFunctionType
AX = mybir.AxisListType
F32 = mybir.dt.float32
F16 = mybir.dt.float16
I32 = mybir.dt.int32
U32 = mybir.dt.uint32

P = 128
HEADS, DH = 16, 32
LN_EPS, RMS_EPS = 1e-5, 1e-6

X_SCALE = 64.0
W_SCALE = 64.0
QK_SCALE = 16.0
V_SCALE = 64.0
P_LOG_SCALE = float(np.log(4096.0))
F_SCALE = 2.0
H_SCALE = 2.0 ** -8
CREDIT = 16


def shape_constants(S):
    slopes = np.array([1.0 / 2 ** (h / 2) for h in range(HEADS)], np.float32)
    tiles = S // P
    a = np.arange(P)[:, None]
    u = np.arange(S)[None, :] - (tiles - 1) * P
    dist = np.where(u > a, -1e30, (u - a) * QK_SCALE * QK_SCALE).astype(np.float32)
    slope = (slopes / (QK_SCALE * QK_SCALE)).astype(np.float32)
    slope = np.append(slope, np.float32(0))
    slope = np.ascontiguousarray(np.broadcast_to(np.concatenate([slope, -slope]), (P, 2 * (HEADS + 1))))
    per_col = (1.0 / np.sqrt(DH)) / np.repeat(slopes.astype(np.float64), DH)
    qcol = (per_col.reshape(4, P).T * QK_SCALE).astype(np.float32)
    kcol = np.full((P, 4), QK_SCALE, np.float32)
    return {
        "dist": dist,
        "slope": slope,
        "col": np.ascontiguousarray(np.concatenate(
            [qcol / (X_SCALE * W_SCALE), kcol / (X_SCALE * W_SCALE), qcol, kcol], axis=1).astype(np.float32)),
        "ident": np.eye(P, dtype=np.float32),
        "ident16": np.eye(P, dtype=np.float16),
    }


def group_schedule(steps, ffn_tiles, subs, first_qk):
    ffn = [("ffn", i, p, 2) for i in range(ffn_tiles) for p in range(2)]
    y = [("y", q, p, 6) for q in range(subs) for p in range(6)]
    qk = [("qk", n, p, 2) for n in range(4) for p in range(2)] if first_qk else []
    weight = [1.0] * steps + ([] if first_qk else [1.7, 1.7])
    per = len(ffn + y + qk) / sum(weight)
    plan, budget, kind = [], 0.0, None
    for s in range(len(weight)):
        budget += weight[s] * per
        plan.append([])
        while (budget >= 0.5 or s == len(weight) - 1) and (ffn or y or qk):
            if kind is None:
                kind = qk if qk and s >= first_qk else ffn or y or qk
            piece = kind.pop(0)
            plan[-1].append(piece)
            budget -= 1.0
            if piece[2] == piece[3] - 1:
                kind = None
                if piece[0] == "ffn" and not ffn:
                    break
    assert not (ffn or y or qk) and all(sum(p[2] == p[3] - 1 for p in now) <= 1 for now in plan)
    return plan


def gated_attention_ffn(nc, x, wqkv, bqkv, wo, bo, gu_packed, gu_scales, dn_packed, dn_scales,
                        dist_t, slope_t, col_t, ident_t, ident16_t, gates, out):
    B, S, D = x.shape
    KT = D // P
    TT = S // P
    F = gu_packed.shape[0] // 2
    FT = F // P
    GROUPS = HEADS * DH // P
    HPG = P // DH
    SUBS = TT // GROUPS
    FW = SUBS * P

    QK_SLOTS = 4
    PRE_SLOTS = QK_SLOTS + TT
    FIRST_ROW = ([("x", t) for t in range(TT)] + [("qk", n) for n in range(QK_SLOTS)]
                 + [("v", t) for t in range(TT)])
    EARLY = TT - 3
    NEXT_ROWS = ([("x", 0)] + [p for t in range(EARLY) for p in (("x", t + 1), ("v", t))]
                 + [("x", t) for t in range(EARLY + 1, TT)] + [("qk", n) for n in range(QK_SLOTS)]
                 + [("v", t) for t in range(EARLY, TT)])
    STEPS = HPG * TT
    SB = PRE_SLOTS + GROUPS * STEPS + TT
    TILE = [i for n in range(TT // 2) for i in (n, TT - 1 - n)]
    UNITS_OF = [1 if i < 4 else 2 for i in TILE]
    UBASE = [sum(UNITS_OF[:i]) for i in range(TT)]
    H_UNITS = sum(UNITS_OF)
    G_UNITS = HPG * H_UNITS
    UB = TT + GROUPS * G_UNITS + TT
    WG = FT + SUBS + 4
    WB = GROUPS * WG - 4
    SP_WIDTH = [max(TILE[k::4]) * P + P for k in range(4)]
    SP_AT = [sum(SP_WIDTH[:k]) for k in range(4)]
    SP = sum(SP_WIDTH)
    assert SB % 2 == 0 and UB % 4 == 0 and PRE_SLOTS % 2 == 0 and STEPS % 4 == 0 and G_UNITS % 4 == 0
    PLAN = {more: group_schedule(STEPS, FT, SUBS, 2 * TT if more else 0) for more in (True, False)}

    def fills(more):
        n, ended = 0, [None]
        for now in PLAN[more]:
            ended.append(None)
            for kind, i, part, parts in now:
                if part == parts - 1:
                    ended[-1] = (n, kind, i)
                    n += 1
        return ended

    ENDED = {more: fills(more) for more in (True, False)}
    assert ENDED[True].pop() == (WG - 1, "y", SUBS - 1)
    CARRIED = (-1, "y", -1)

    def fill_of(prev, more, s):
        return CARRIED if prev and s == 0 else ENDED[more][s]

    BANK = [n % 2 if n < FT - 1 else (n - 1) % 2 for n in range(WG)]

    def bank_read(n):
        return 1 + max(m for m in range(-2, n) if (BANK[m] if m >= 0 else -m % 2) == BANK[n])

    def units_before(s):
        return s // TT * H_UNITS + UBASE[s % TT]

    def tanhs(kind, i):
        return i + 1 if kind == "ffn" else i // SUBS * (FT + SUBS) + FT + i % SUBS + 1

    def units_of(s):
        return range(units_before(s), units_before(s + 1))

    with ExitStack() as ctx:
        def sb(name, shape, dt):
            return ctx.enter_context(nc.sbuf_tensor(name, shape, dt))

        def sem(name):
            return ctx.enter_context(nc.semaphore(name))

        wqkv_sb = sb("wqkv_sb", [P, 2, KT, 3 * D], F16)
        wo_sb = sb("wo_sb", [P, 2, KT, D], F16)
        wgu_sb = sb("wgu_sb", [P, 2, KT, 2 * F], F16)
        wdn_sb = sb("wdn_sb", [P, 2, FT, D], F16)
        xT = sb("xT", [P, 2, KT, S], F16)
        vals = sb("vals", [P, TT, HEADS * 2 * DH], F16)
        vals_v = vals[:, :, :].rearrange("p t (h c d) -> p t h c d", h=HEADS, c=2)
        xo = sb("xo", [P, TT, D], F32)
        QN, Q4, K4 = SP, SP + 2 * S, SP + 3 * S
        att = sb("att", [P, SP + 4 * S], F32)
        scores_of = [att[:, SP_AT[k % 4]:SP_AT[k % 4] + (i + 1) * P] for k, i in enumerate(TILE)]
        qk_nat = att[:, QN:Q4].bitcast(F16).rearrange("p (t c s) -> p t c s", t=2, c=2)
        q4 = att[:, Q4:K4].bitcast(F16).rearrange("p (n s) -> p n s", n=2)
        k4 = att[:, K4:K4 + S].bitcast(F16).rearrange("p (n s) -> p n s", n=2)
        x_buf = att[:, 0:TT * D].rearrange("p (t d) -> p t d", t=TT)
        xr = att[:, Q4:Q4 + 4 * D].rearrange("p (n d) -> p n d", n=4)
        hT = sb("hT", [P, 2, FT, FW], F16)
        gr = hT[:, :, :, :].rearrange("p c k t -> p (c k t)")[:, 0:8 * D].bitcast(F32).rearrange("p (n d) -> p n d", n=4)
        pt_sb = sb("pt_sb", [P, 4, 2, 512], F16)
        dist = sb("dist", [P, S], F32)
        tmp = sb("tmp", [P, 3 * 512], F32)
        tf = tmp[:, 0:512]
        th = tmp[:, 512:1024]
        gst = tmp[:, 1024:1536]
        bo_sb = sb("bo_sb", [P, D], F32)
        ored = sb("ored", [P, TT, DH], F32)
        ident = sb("ident", [P, P], F32)
        slope = sb("slope", [P, 2 * (HEADS + 1)], F32)
        slope_v = slope[:, :].rearrange("p (c h) -> p c h", c=2)
        gslope = sb("gslope", [P, 2, HPG + 1], F32)
        col = sb("col", [P, 16], F32)
        colb = sb("colb", [P, 8], F32)
        stats = sb("stats", [P, TT, 6], F32)
        mv = sb("mv", [P, TT, 2], F32)
        base = sb("base", [P, TT], F32)
        rstd = sb("rstd", [P, TT], F32)
        neghalf = sb("neghalf", [P, TT], F32)
        mx = sb("mx", [P, 4], F32)
        nm = sb("nm", [P, 4], F32)
        sums = sb("sums", [P, 2, TT], F32)
        rsum = sb("rsum", [P, TT], F32)
        ssq = sb("ssq", [P, SUBS], F32)
        rbase = sb("rbase", [P, SUBS], F32)
        rr = sb("rr", [P, SUBS], F32)

        longs = ctx.enter_context(nc.psum_tensor("longs", [P, 1024], F32))
        shorts = ctx.enter_context(nc.psum_tensor("shorts", [P, 512], F32))
        pt = [ctx.enter_context(nc.psum_tensor(f"pt{i}", [P, 512], F32)) for i in range(2)]
        three = [shorts[:, :], longs[:, 0:512], longs[:, 512:1024]]
        ops = ctx.enter_context(nc.psum_tensor("ops", [P, TT * 2 * DH], F32))
        work = [ctx.enter_context(nc.psum_tensor(f"work{i}", [P, 512], F32)) for i in range(2)]

        GU_T = 2 * FT
        DN_T = D // P
        WORDS = D // 8
        DN_WORDS = F // 8
        xo_f = xo[:, :, :].rearrange("p t d -> p (t d)")
        wo_in = att[:, TT * D:TT * D + KT * D].rearrange("p (k d) -> p k d", k=KT)
        gu_in = xo_f[:, 2048:2048 + GU_T * WORDS].bitcast(U32).rearrange("p (t w) -> p t w", t=GU_T)
        signs = xo_f[:, 0:1024].bitcast(U32).rearrange("p (k w) -> p k w", k=4)
        mags = [a.bitcast(U32).rearrange("p (k w) -> p k w", k=4) for a in (xo_f[:, 1024:2048], dist[:, :])]
        dn_in = tmp[:, 512:512 + DN_T * DN_WORDS].bitcast(U32).rearrange("p (t w) -> p t w", t=DN_T)
        vals_f = vals[:, :, :].rearrange("p t n -> p (t n)").bitcast(F32)
        xT_f = xT[:, :, :, :].rearrange("p c k t -> p (c k t)").bitcast(F32)
        wqkv_in = [a[:, n * 3 * D:(n + 1) * 3 * D] for a in (vals_f, xT_f) for n in range(2)]
        hT_f = hT[:, :, :, :].rearrange("p c k t -> p (c k t)").bitcast(F32)
        wf = [pt_sb[:, :, :, :].rearrange("p a b c -> p (a b c)").bitcast(F32), hT_f[:, 0:2048]]
        gus_in = hT_f[:, 0:GU_T * P // 2].bitcast(F16)[0:KT, :]
        dns_in = hT_f[:, 1408:1408 + D // 2].bitcast(F16)[0:FT, :]
        assert GU_T * P // 2 <= 1408 and 1408 + D // 2 <= 2048

        batches = []
        for t0 in range(0, GU_T, 4):
            n = min(4, GU_T - t0)
            batches.append((gu_in[:, t0:t0 + n, :], t0 * KT, n, KT,
                            [[wgu_sb[:, c, g, t0 * P:(t0 + n) * P] for c in range(2)] for g in range(KT)]))
        scale0 = GU_T * KT
        for g0 in range(0, FT, 4):
            ng = min(4, FT - g0)
            batches.append((dn_in[:, :, g0 * 16:(g0 + ng) * 16], scale0, DN_T, ng,
                            [[wdn_sb[:, c, g0 + g, :] for c in range(2)] for g in range(ng)]))
            scale0 += DN_T * ng
        scl = hT_f[:, 2048:2048 + scale0]
        ident16 = hT_f[:, 2200:2208].bitcast(F16)[0:16, :]
        bv_in = hT_f[:, 2210:2210 + KT]
        bv_rows = hT_f[:, 2220:2220 + KT * P].bitcast(F16).rearrange("p (c k m) -> p c k m", c=2, k=KT)
        banks = [work[0][:, :], work[1][:, :], ops[:, :], pt[0][:, :], pt[1][:, :]]
        first_of = [sum(x[3] for x in batches[:k]) for k in range(len(batches) + 1)]

        def decoding_beside(r, decode, finish):
            if r + 1 < len(batches):
                finish(r + 1)
            if r + 3 < len(batches):
                decode(r + 3)

        w_in = [sem(f"w_in{k}") for k in range(KT)]
        wo_loaded = sem("wo_loaded")
        gu_loaded = sem("gu_loaded")
        dn_loaded = sem("dn_loaded")
        scales_in = sem("scales_in")
        ident_in = sem("ident_in")
        small_in = sem("small_in")
        dist_in = sem("dist_in")
        split_hi = sem("split_hi")
        split_lo = sem("split_lo")
        scales_t = sem("scales_t")
        bias_done = sem("bias_done")
        bv_done = sem("bv_done")
        bv_wo = sem("bv_wo")
        scl_done = sem("scl_done")
        bits = sem("bits")
        codes = sem("codes")
        wf_done = sem("wf_done")
        bank_full = sem("bank_full")
        bank_hi = sem("bank_hi")
        bank_lo = sem("bank_lo")

        x_in = sem("x_in")
        bn_done = sem("bn_done")
        mv_done = sem("mv_done")
        base_done = sem("base_done")
        rstd_done = sem("rstd_done")
        xn_done = sem("xn_done")
        slot_full = sem("slot_full")
        slot_free = sem("slot_free")
        unit_full = sem("unit_full")
        unit_hi = sem("unit_hi")
        unit_lo = sem("unit_lo")
        unit_used = sem("unit_used")
        work_full = sem("work_full")
        work_free = sem("work_free")
        v_hi = sem("v_hi")
        qk_hi = sem("qk_hi")
        qk_f32 = sem("qk_f32")
        qk_lo = sem("qk_lo")
        q4_in = [sem("q4_in0"), sem("q4_in1")]
        gslope_done = sem("gslope_done")
        nm_done = sem("nm_done")
        exp_done = sem("exp_done")
        o_read = sem("o_read")
        rsum_done = sem("rsum_done")
        o_norm = sem("o_norm")
        th_done = sem("th_done")
        ga_done = sem("ga_done")
        h_hi = sem("h_hi")
        h_lo = sem("h_lo")
        ss_done = sem("ss_done")
        rb_done = sem("rb_done")
        rr_done = sem("rr_done")
        g_done = sem("g_done")
        g_out = sem("g_out")
        xr_in = [sem(f"xr_in{n}") for n in range(4)]
        gated = sem("gated")
        res = sem("res")
        out_done = [sem(f"out_done{n}") for n in range(4)]
        held = {e: sem(f"held_{e}") for e in ("act", "dve", "pe", "pool", "sp")}

        x_t = x.rearrange("b (t p) d -> p (b t) d", p=P)
        x_rows = x.rearrange("b s d -> (b s) d")
        out_rows = out.rearrange("b s d -> (b s) d")

        block = ctx.enter_context(nc.Block())
        C = CREDIT

        def hold(eng, name, semaphore, value):
            eng.wait_ge(semaphore, value)
            eng.sem_inc(held[name], 1)

        @block.sync
        def _(sp):
            def load_tokens(b):
                sp.dma_start(x_buf[:, :, :], x_t[:, bass.ds(b * TT, TT), :]).then_inc(x_in, 16)

            def stack_head(b, g, j):
                if j == 0:
                    hold(sp, "sp", qk_lo, (b * GROUPS + g) * 4 + (4 + C))
                hold(sp, "sp", slot_full, b * SB + g * STEPS + (PRE_SLOTS + (j - 1) * TT + C))
                rows = slice(DH * j, DH * j + DH)
                for quarter in range(4):
                    place = slice(DH * quarter, DH * quarter + DH)
                    sp.dma_start(q4[place, j % 2, :], qk_nat[rows, 0, quarter // 2, :]).then_inc(q4_in[j % 2], 16)
                    sp.dma_start(k4[place, j % 2, :], qk_nat[rows, 1, quarter % 2, :]).then_inc(q4_in[j % 2], 16)

            def store_gates(b, g, q):
                hold(sp, "sp", g_done, (b * GROUPS + g) * SUBS + (q + 1 + C))
                sp.dma_start(gates[bass.ds((b * TT + g * SUBS + q) * P, P), :], gst[:, :]).then_inc(g_out, 16)

            def row(b, last):
                for n in range(4):
                    hold(sp, "sp", out_done[n], b * (TT // 4 * 16) + 16)
                for j in range(HPG):
                    stack_head(b, 0, j)
                with sp.Fori(0, GROUPS - 1) as g:
                    stack_head(b, g + 1, 0)
                    store_gates(b, g, 0)
                    stack_head(b, g + 1, 1)
                    store_gates(b, g, 1)
                    stack_head(b, g + 1, 2)
                    stack_head(b, g + 1, 3)
                store_gates(b, GROUPS - 1, 0)
                hold(sp, "sp", slot_full, b * SB + (PRE_SLOTS + GROUPS * STEPS + C))
                hold(sp, "sp", unit_full, b * UB + (TT + GROUPS * G_UNITS + C))
                if not last:
                    load_tokens(b + 1)
                def load(n):
                    sp.dma_start(xr[:, n % 4, :], x_rows[bass.ds(b * S + n * P, P), :]).then_inc(xr_in[n % 4], 16)
                    sp.dma_start(gr[:, n % 4, :], gates[bass.ds(b * S + n * P, P), :]).then_inc(xr_in[n % 4], 16)

                hold(sp, "sp", work_full, b * WB + (WB + C))
                hold(sp, "sp", g_out, b * (TT * 16) + TT * 16)
                for n in range(3):
                    load(n)
                store_gates(b, GROUPS - 1, 1)
                for n in range(TT):
                    if n + 3 < TT:
                        if n >= 1:
                            hold(sp, "sp", out_done[(n - 1) % 4], b * (TT // 4 * 16) + ((n - 1) // 4 * 16 + 32))
                        if n + 3 == TT - 1:
                            hold(sp, "sp", g_out, b * (TT * 16) + (TT * 16 + 16))
                        load(n + 3)
                    hold(sp, "sp", res, b * TT + (n + 1 + C))
                    sp.dma_start(out_rows[bass.ds(b * S + n * P, P), :], xr[:, n % 4, :]).then_inc(out_done[n % 4], 16)

            for n in range(4):
                sp.sem_inc(out_done[n], 16)
            sp.sem_inc(g_out, 16)
            sp.dma_start(gus_in, gu_scales).then_inc(scales_in, 16)
            sp.dma_start(dns_in, dn_scales).then_inc(scales_in, 16)
            sp.dma_start(ident16, ident16_t[0:16, 0:16]).then_inc(scales_in, 16)
            sp.dma_start(gu_in, gu_packed.bitcast(U32).rearrange("(t p) w -> p t w", p=P)).then_inc(gu_loaded, 16)
            load_tokens(0)
            for k in range(KT):
                sp.dma_start(wqkv_in[k], wqkv[k * P:(k + 1) * P, :]).then_inc(w_in[k], 16)
            sp.dma_start(wo_in, wo.rearrange("(k p) d -> p k d", p=P)).then_inc(wo_loaded, 16)
            sp.dma_start(dn_in, dn_packed.bitcast(U32).rearrange("(t p) w -> p t w", p=P)).then_inc(dn_loaded, 16)
            with sp.Fori(0, B - 1) as b:
                row(b, False)
            row(B - 1, True)
            sp.wait_ge(g_out, B * TT * 16 + 16)
            for n in range(4):
                sp.wait_ge(out_done[n], B * (TT // 4 * 16) + 16)

        @block.gpsimd
        def _(pool):
            for s in (nm_done, o_norm, h_lo, rstd_done, rr_done, gated, res):
                pool.sem_inc(s, C)

            def token_scales(b):
                pool.wait_ge(base_done, b + (1 + C))
                nc.gpsimd.tensor_tensor(rstd[:, :], base[:, :], neghalf[:, :], ALU.pow).then_inc(rstd_done, 1)

            def exponent_bias(gs, s, neg_slope):
                hold(pool, "pool", slot_free, gs + (s + 1 + C))
                nc.gpsimd.tensor_scalar(nm[:, s % 4:s % 4 + 1], mx[:, s % 4:s % 4 + 1], neg_slope, P_LOG_SCALE,
                                        ALU.mult, ALU.add).then_inc(nm_done, 1)

            def group(b, g, prev, more):
                gs = pool.snap(b * SB + g * STEPS + PRE_SLOTS)
                it = pool.snap(b * GROUPS + g)
                for s in range(STEPS + (0 if more else 3)):
                    if s + 1 < STEPS + more:
                        j = (s + 1) // TT
                        exponent_bias(gs, s + 1, gslope[:, 1, j:j + 1])
                    n, kind, i = fill_of(prev, more, s) or (0, None, 0)
                    if kind == "ffn":
                        pool.wait_ge(h_hi, it * FT + (i + 1 + C))
                        nc.gpsimd.tensor_tensor(hT[:, 1, i, :], th[:, i % 2 * FW:(i % 2 + 1) * FW], hT[:, 0, i, :],
                                                ALU.subtract).then_inc(h_lo, 1)
                    elif kind == "y":
                        q = i % SUBS
                        pool.wait_ge(rb_done, it * SUBS + (i + 1 + C))
                        nc.gpsimd.tensor_tensor(rr[:, q:q + 1], rbase[:, q:q + 1], neghalf[:, 0:1],
                                                ALU.pow).then_inc(rr_done, 1)
                    if s > TT and s % TT == 1 or prev and s == 1:
                        j = s // TT - 1
                        pool.wait_ge(rsum_done, it * HPG + (j + 1 + C))
                        pool.wait_ge(o_read, it * HPG + (j + 1 + C))
                        nc.gpsimd.tensor_tensor(xo[:, :, bass.ds((g * HPG + j) * DH, DH)], ored[:, :, :],
                                                rsum[:, :].unsqueeze(2).broadcast_to([P, TT, DH]),
                                                ALU.mult).then_inc(o_norm, 1)

            def row(b, last):
                exponent_bias(pool.snap(b * SB + PRE_SLOTS), 0, slope_v[:, 1, 0:1])
                pool.wait_ge(res, b * TT + C)
                group(b, 0, False, True)
                with pool.Fori(1, GROUPS - 1) as g:
                    group(b, g, True, True)
                group(b, GROUPS - 1, True, False)
                for n in range(TT):
                    if n == 3 and not last:
                        token_scales(b + 1)
                    pool.wait_ge(slot_free, b * SB + (PRE_SLOTS + GROUPS * STEPS + n + 1 + C))
                    pool.wait_ge(xr_in[n % 4], b * (TT // 4 * 32) + (n // 4 + 1) * 32)
                    nc.gpsimd.tensor_tensor(gr[:, n % 4, :], xo[:, n, :], gr[:, n % 4, :], ALU.mult).then_inc(gated, 1)
                    pool.wait_ge(gated, b * TT + (n + 1 + C))
                    nc.gpsimd.tensor_tensor(xr[:, n % 4, :], gr[:, n % 4, :], xr[:, n % 4, :], ALU.add).then_inc(res, 1)

            for k, (_, s0, no, ng, _) in enumerate(batches):
                if k == 2:
                    token_scales(0)
                pool.wait_ge(codes, k + 1)
                if k >= 2:
                    pool.wait_ge(bank_full, first_of[k - 1])
                blocks = no * ng
                for q in range(4):
                    nc.gpsimd.tensor_tensor(
                        wf[k % 2][:, 0:blocks * P].rearrange("p (b w e) -> p b w e", b=blocks, e=8)[:, :, :, q::4],
                        mags[k % 2][:, q, 0:blocks * 16].bitcast(F16).rearrange("p (b w e) -> p b w e", b=blocks, e=2),
                        scl[:, s0:s0 + blocks].unsqueeze(2).unsqueeze(3).broadcast_to([P, blocks, 16, 2]),
                        ALU.mult).then_inc(wf_done, 1)
                if k == len(batches) // 2 * 2 - 1:
                    pool.wait_ge(wf_done, 4 * (k + 1))
                    pool.dma_start(dist[:, :], dist_t).then_inc(dist_in, 16)
            with pool.Fori(0, B - 1) as b:
                row(b, False)
            row(B - 1, True)

        @block.tensor
        def _(pe):
            for s in (slot_full, unit_full, unit_used, work_full):
                pe.sem_inc(s, C)

            def fill_transposes(u0, u, source, blocks):
                pe.wait_ge(unit_lo, u0 + (u - 1 + C))
                for i in range(blocks):
                    mm = nc.tensor.transpose(pt[u % 2][:, i * P:(i + 1) * P], source(i), ident[:, :])
                mm.then_inc(unit_full, 1)

            def products(dst, pairs, part=0, parts=1):
                terms = [(l[a], r[c]) for l, r in pairs for a, c in ((0, 0), (0, 1), (1, 0))]
                n = len(terms)
                for i in range(part * n // parts, (part + 1) * n // parts):
                    mm = nc.tensor.matmul(dst, *terms[i], start=(i == 0), stop=(i == n - 1))
                return mm

            def qk_pairs(g, t, half):
                return [([wqkv_sb[:, c, k, bass.ds(g * P + t * D, P)] for c in range(2)],
                         [xT[:, c, k, half * 512:(half + 1) * 512] for c in range(2)]) for k in range(KT)]

            def scores(gs, it, s):
                j, i = divmod(s, TT)
                if i == 0:
                    pe.wait_ge(q4_in[j % 2], it * 256 + (j // 2 + 1) * 128)
                pe.wait_ge(slot_free, gs + (s - 1 + C))
                i = TILE[i]
                width = (i + 1) * P
                for c in range(0, width, 512):
                    e = min(c + 512, width)
                    mm = nc.tensor.matmul((shorts, longs)[s % 2][:, c:e], q4[:, j % 2, i * P:(i + 1) * P],
                                          k4[:, j % 2, c:e], start=True, stop=True)
                mm.then_inc(slot_full, 1)

            def group(b, g, prev, more):
                gs = pe.snap(b * SB + g * STEPS + PRE_SLOTS)
                gu = pe.snap(b * UB + g * G_UNITS + TT)
                gw = pe.snap(b * WB + g * WG)
                it = pe.snap(b * GROUPS + g)

                def transposes(s):
                    pe.wait_ge(exp_done, it * STEPS + (s + 1 + C))
                    for n, u in enumerate(units_of(s)):
                        fill_transposes(gu, u, lambda q: scores_of[s % TT][:, (4 * n + q) * P:(4 * n + q + 1) * P],
                                        min(4, TILE[s % TT] + 1 - 4 * n))

                def times_values(s):
                    j, i = divmod(s, TT)
                    if i == 0:
                        pe.wait_ge(o_read, it * HPG + (j + C))
                    i = TILE[i]
                    for n, u in enumerate(units_of(s)):
                        pe.wait_ge(unit_lo, gu + (u + 1 + C))
                        for q in range(min(4, i + 1 - 4 * n)):
                            t = 4 * n + q
                            for c in range(2):
                                mm = nc.tensor.matmul(
                                    ops[:, i * 64:(i + 1) * 64], pt_sb[:, u % 4, c, q * P:(q + 1) * P],
                                    vals[:, t, bass.ds((g * HPG + j) * 2 * DH, 2 * DH)],
                                    start=(t == 0 and c == 0), stop=(t == i and c == 1))
                        mm.then_inc(unit_used, 1)

                def piece(n, kind, i, part, parts):
                    bank = work[BANK[n]]
                    if part == 0:
                        pe.wait_ge(work_free, gw + (bank_read(n) + C))
                    if kind == "ffn":
                        c0 = part * F + i * P
                        mm = products(bank[:, part * FW:(part + 1) * FW], [
                            ([wgu_sb[:, c, k, c0:c0 + P] for c in range(2)],
                             [xT[:, c, k, bass.ds(g * FW, FW)] for c in range(2)]) for k in range(KT)])
                    elif kind == "y":
                        if part == 0 and i == 0:
                            pe.wait_ge(h_lo, it * FT + (FT + C))
                        mm = products(bank[:, :], [
                            ([hT[:, c, k, i * P:(i + 1) * P] for c in range(2)],
                             [wdn_sb[:, c, k, :] for c in range(2)]) for k in range(FT)], part, parts)
                    else:
                        mm = products(bank[:, :], qk_pairs(g + 1, i // 2, i % 2), part, parts)
                    if part == parts - 1:
                        mm.then_inc(work_full, 1)

                n = 0
                for s in range(STEPS if more else STEPS + 2):
                    if (prev or s >= 1) and s <= STEPS:
                        transposes(s - 1)
                    late = s >= 2 and (s - 2) % TT == 0
                    if (prev or s >= 2) and not late:
                        times_values(s - 2)
                    if s + 2 < STEPS or more and s < STEPS:
                        scores(gs, it, s + 2)
                    for kind, i, part, parts in PLAN[more][s]:
                        piece(n, kind, i, part, parts)
                        n += part == parts - 1
                    if late:
                        times_values(s - 2)

            def prepare(b, beside=None):
                sl = pe.snap(b * SB)
                un = pe.snap(b * UB)
                r = 0
                for kind, i in FIRST_ROW if beside else NEXT_ROWS:
                    if kind == "x":
                        pe.wait_ge(xn_done, b * TT + (i + 1 + C))
                        fill_transposes(un, i, lambda k: x_buf[:, i, k * P:(k + 1) * P], KT)
                        continue
                    pe.wait_ge(slot_free, sl + (max(r - 2, 0) + C))
                    if kind == "qk":
                        pe.wait_ge(unit_lo, un + (TT + C))
                        mm = products(three[r % 3], qk_pairs(0, i // 2, i % 2))
                    else:
                        pe.wait_ge(unit_lo, un + (i + 1 + C))
                        mm = products(three[r % 3], [
                            ([xT[:, c, k, i * P:(i + 1) * P] for c in range(2)],
                             [wqkv_sb[:, c, k, 2 * D:3 * D] for c in range(2)]) for k in range(KT)])
                    mm.then_inc(slot_full, 1)
                    if beside:
                        beside(r)
                    r += 1

            def row(b, last):
                sl = pe.snap(b * SB)
                un = pe.snap(b * UB)
                for s in range(2):
                    scores(sl + PRE_SLOTS, b * GROUPS, s)
                hold(pe, "pe", slot_free, sl + (PRE_SLOTS + C))
                group(b, 0, False, True)
                with pe.Fori(1, GROUPS - 1) as g:
                    group(b, g, True, True)
                group(b, GROUPS - 1, True, False)

                def turn_output(n):
                    if n == 0:
                        pe.wait_ge(o_norm, b * HEADS + (HEADS + C))
                    fill_transposes(un, TT + GROUPS * G_UNITS + n, lambda i: xo[:, n, i * P:(i + 1) * P], KT)

                turn_output(0)
                for n in range(TT):
                    if n + 1 < TT:
                        turn_output(n + 1)
                    pe.wait_ge(slot_free, sl + (PRE_SLOTS + GROUPS * STEPS + max(n - 2, 0) + C))
                    pe.wait_ge(unit_lo, un + (TT + GROUPS * G_UNITS + n + 1 + C))
                    products(three[n % 3], [
                        ([pt_sb[:, n % 4, c, k * P:(k + 1) * P] for c in range(2)],
                         [wo_sb[:, c, k, :] for c in range(2)]) for k in range(KT)]).then_inc(slot_full, 1)
                if not last:
                    prepare(b + 1)

            def transpose_batch(k):
                _, _, no, ng, _ = batches[k]
                pe.wait_ge(wf_done, 4 * (k + 1))
                for g in range(ng):
                    n = first_of[k] + g
                    if n >= 5:
                        pe.wait_ge(bank_lo, n - 4)
                    for i in range(no):
                        a = (i * ng + g) * P
                        mm = nc.tensor.transpose(banks[n % 5][:, i * P:(i + 1) * P], wf[k % 2][:, a:a + P], ident[:, :])
                    mm.then_inc(bank_full, 1)

            pe.wait_ge(scales_in, 16 * 3)
            pg = work[0][:, :].bitcast(F16)
            for t in range(GU_T):
                nc.tensor.transpose(pg[:, t * KT:(t + 1) * KT], gus_in[:, t * P:(t + 1) * P], ident16[0:KT, 0:KT])
            pd = work[1][:, :].bitcast(F16)
            for t in range(DN_T):
                mm = nc.tensor.transpose(pd[:, t * 16:t * 16 + FT], dns_in[:, t * P:(t + 1) * P], ident16[0:FT, 0:FT])
            mm.then_inc(scales_t, 1)
            pe.wait_ge(ident_in, 16)
            transpose_batch(0)
            pe.wait_ge(split_lo, KT)
            pe.wait_ge(bank_lo, first_of[1])
            prepare(0, lambda r: decoding_beside(r, lambda k: None, transpose_batch))
            pe.wait_ge(bv_done, 2)
            pe.wait_ge(split_lo, 1 + KT)
            pe.wait_ge(bank_lo, first_of[-1])
            products(ops[:, :], [([bv_rows[:, a, k, :] for a in range(2)], [wo_sb[:, c, k, :] for c in range(2)])
                                 for k in range(KT)]).then_inc(bv_wo, 1)
            pe.wait_ge(bias_done, 2)
            with pe.Fori(0, B - 1) as b:
                row(b, False)
            row(B - 1, True)

        @block.scalar
        def _(act):
            for s in (unit_hi, v_hi, qk_f32, qk_hi, exp_done, th_done, h_hi, ss_done):
                act.sem_inc(s, C)

            def unit_to_hi(u0, u, dst, width, rows):
                act.wait_ge(unit_full, u0 + (u + 1 + C))
                src = pt[u % 2][:, 0:width]
                if rows:
                    src = src.rearrange("p (k t) -> p k t", k=rows)
                nc.scalar.copy(dst, src).then_inc(unit_hi, 1)

            def qk_in_f32(it, g, n, src, full, value):
                t = n // 2
                hold(act, "act", full, value)
                hold(act, "act", qk_lo, it * 4 + (n + C))
                nc.scalar.activation(tf[:, :], src, ACT.Identity, bias=colb[:, bass.ds(g + 4 * t, 1)],
                                     scale=col[:, bass.ds(g + 4 * t, 1)]).then_inc(qk_f32, 1)

            def qk_to_hi(it, n):
                act.wait_ge(qk_f32, it * 4 + (n + 1 + C))
                nc.scalar.copy(qk_nat[:, n // 2, 0, n % 2 * 512:(n % 2 + 1) * 512], tf[:, :]).then_inc(qk_hi, 1)

            def group(b, g, prev, more):
                gu = act.snap(b * UB + g * G_UNITS + TT)
                gw = act.snap(b * WB + g * WG)
                it = act.snap(b * GROUPS + g)
                gth = act.snap(it * (FT + SUBS))

                def exponent(s):
                    j, k = divmod(s, TT)
                    if s == 0:
                        act.wait_ge(gslope_done, it + (1 + C))
                    act.wait_ge(nm_done, it * STEPS + (s + 1 + C))
                    nc.scalar.activation(scores_of[k], scores_of[k], ACT.Exp,
                                         bias=nm[:, s % 4:s % 4 + 1], scale=gslope[:, 0, j:j + 1],
                                         accum_out=sums[:, j % 2, TILE[k]:TILE[k] + 1]).then_inc(exp_done, 1)

                def first_read(n, kind, i):
                    bank = work[BANK[n]]
                    if kind == "ffn":
                        act.wait_ge(work_full, gw + (n + 1 + C))
                        if i < 2:
                            act.wait_ge(g_done, it * SUBS + C)
                        else:
                            act.wait_ge(h_lo, it * FT + (i - 1 + C))
                        nc.scalar.activation(th[:, i % 2 * FW:(i % 2 + 1) * FW], bank[:, 0:FW], ACT.Tanh,
                                             scale=0.5 / (X_SCALE * F_SCALE)).then_inc(th_done, 1)
                    elif kind == "y":
                        act.wait_ge(work_full, gw + (n + 1 + C))
                        if i == 0:
                            act.wait_ge(h_lo, it * FT + (FT + C))
                        else:
                            act.wait_ge(g_done, it * SUBS + (i + C))
                        nc.scalar.activation(th[:, :], bank[:, :], ACT.Square,
                                             accum_out=ssq[:, i % SUBS:i % SUBS + 1]).then_inc(ss_done, 1)
                    else:
                        if i == 0:
                            for parity in range(2):
                                hold(act, "act", q4_in[parity], it * 256 + 256)
                        qk_in_f32(it + 1, g + 1, i, bank[:, :], work_full, gw + (n + 1 + C))

                def second_read(n, kind, i):
                    if kind == "ffn":
                        act.wait_ge(work_free, gw + (n + 1 + C))
                        nc.scalar.copy(hT[:, 0, i, :], th[:, i % 2 * FW:(i % 2 + 1) * FW]).then_inc(h_hi, 1)
                    elif kind == "y":
                        act.wait_ge(ss_done, it * SUBS + (i + 1 + C))
                        act.wait_ge(rr_done, it * SUBS + (i + 1 + C))
                        nc.scalar.activation(th[:, :], work[BANK[n]][:, :], ACT.Tanh,
                                             scale=rr[:, i % SUBS:i % SUBS + 1]).then_inc(th_done, 1)
                    else:
                        qk_to_hi(it + 1, i)

                for s in range(STEPS if more else STEPS + 2):
                    fill = fill_of(prev, more, s)
                    if fill:
                        first_read(*fill)
                    if (prev or s >= 1) and s <= STEPS:
                        for n, u in enumerate(units_of(s - 1)):
                            w = min(4, TILE[(s - 1) % TT] + 1 - 4 * n) * P
                            act.wait_ge(unit_used, it * G_UNITS + (u - 3 + C))
                            unit_to_hi(gu, u, pt_sb[:, u % 4, 0, 0:w], w, 0)
                    if s < STEPS:
                        exponent(s)
                    if fill:
                        second_read(*fill)

                def last_gates():
                    first_read(*ENDED[False][STEPS + 2])
                    second_read(*ENDED[False][STEPS + 2])

                return last_gates

            def prepare(b, beside=None):
                un = act.snap(b * UB)
                sl = act.snap(b * SB)
                r = 0
                for kind, i in FIRST_ROW if beside else NEXT_ROWS:
                    if kind == "x":
                        unit_to_hi(un, i, xT[:, 0, :, i * P:(i + 1) * P], KT * P, KT)
                        continue
                    if kind == "qk":
                        qk_in_f32(b * GROUPS, 0, i, three[r % 3], slot_full, sl + (r + 1 + C))
                        qk_to_hi(b * GROUPS, i)
                    else:
                        act.wait_ge(slot_full, sl + (r + 1 + C))
                        nc.scalar.activation(vals_v[:, i, :, 0, :],
                                             three[r % 3].rearrange("p (h d) -> p h d", h=HEADS),
                                             ACT.Copy, scale=V_SCALE / (X_SCALE * W_SCALE)).then_inc(v_hi, 1)
                    if beside:
                        beside(r)
                    r += 1

            def row(b, last):
                un = act.snap(b * UB)
                act.wait_ge(res, b * TT + C)
                group(b, 0, False, True)
                with act.Fori(1, GROUPS - 1) as g:
                    group(b, g, True, True)
                last_gates = group(b, GROUPS - 1, True, False)
                for n in range(TT):
                    unit_to_hi(un, TT + GROUPS * G_UNITS + n, pt_sb[:, n % 4, 0, :], 512, 0)
                    if n == 1:
                        last_gates()
                if not last:
                    prepare(b + 1)

            act.dma_start(ident[:, :], ident_t).then_inc(ident_in, 16)
            act.dma_start(slope[:, :], slope_t).then_inc(small_in, 16)
            act.dma_start(col[:, :], col_t).then_inc(small_in, 16)
            with nc.allow_non_contiguous_dma(reason="1024 biases, once"):
                act.dma_start(colb[:, :], bqkv[0:2 * D].rearrange("(t p) -> p t", p=P)).then_inc(small_in, 16)
                act.dma_start(bv_in, bqkv[2 * D:3 * D].rearrange("(t p) -> p t", p=P)).then_inc(small_in, 16)
            act.dma_start(bo_sb[:, :], bo.partition_broadcast(P)).then_inc(small_in, 16)

            def split(source, hi, loaded):
                act.wait_ge(loaded, 16)
                nc.scalar.activation(hi, source, ACT.Copy, scale=W_SCALE).then_inc(split_hi, 1)

            def batch_to_hi(k):
                _, _, no, ng, dst = batches[k]
                for g in range(ng):
                    n = first_of[k] + g
                    act.wait_ge(bank_full, n + 1)
                    nc.scalar.copy(dst[g][0], banks[n % 5][:, 0:no * P]).then_inc(bank_hi, 1)

            batch_to_hi(0)
            for k in range(KT):
                split(wqkv_in[k], wqkv_sb[:, 0, k, :], w_in[k])
            split(wo_in, wo_sb[:, 0, :, :], wo_loaded)
            act.wait_ge(split_lo, 1 + KT)
            act.wait_ge(bias_done, 1)
            prepare(0, lambda r: decoding_beside(r, lambda k: None, batch_to_hi))
            with act.Fori(0, B - 1) as b:
                row(b, False)
            row(B - 1, True)

        @block.vector
        def _(dve):
            for s in (bn_done, mv_done, base_done, xn_done, slot_free, unit_lo, work_free, qk_lo, gslope_done,
                      o_read, rsum_done, ga_done, rb_done, g_done):
                dve.sem_inc(s, C)

            def unit_to_lo(u0, u, dst, hi, width, rows):
                dve.wait_ge(unit_hi, u0 + (u + 1 + C))
                src = pt[u % 2][:, 0:width]
                if rows:
                    src = src.rearrange("p (k t) -> p k t", k=rows)
                nc.vector.tensor_tensor(dst, src, hi, ALU.subtract).then_inc(unit_lo, 1)

            def qk_to_lo(it, n):
                t, half = divmod(n, 2)
                cols = slice(half * 512, (half + 1) * 512)
                dve.wait_ge(qk_hi, it * 4 + (n + 1 + C))
                nc.vector.tensor_tensor(qk_nat[:, t, 1, cols], tf[:, :], qk_nat[:, t, 0, cols],
                                        ALU.subtract).then_inc(qk_lo, 1)

            def masked_max(gs, gu, s):
                k = s % TT
                width = (TILE[k] + 1) * P
                dve.wait_ge(unit_full, gu + (units_before(s - 3) + C))
                hold(dve, "dve", slot_full, gs + (s + 1 + C))
                nc.vector.tensor_tensor_reduce(scores_of[k], (shorts, longs)[s % 2][:, 0:width],
                                               dist[:, S - width:S], 1.0, -3e38, ALU.add, ALU.max,
                                               mx[:, s % 4:s % 4 + 1]).then_inc(slot_free, 1)

            def group(b, g, prev, more):
                gs = dve.snap(b * SB + g * STEPS + PRE_SLOTS)
                gu = dve.snap(b * UB + g * G_UNITS + TT)
                gw = dve.snap(b * WB + g * WG)
                it = dve.snap(b * GROUPS + g)
                gth = dve.snap(it * (FT + SUBS))
                dve.wait_ge(exp_done, it * STEPS + C)
                dve.wait_ge(nm_done, it * STEPS + (1 + C))
                nc.vector.tensor_copy(gslope[:, :, :], slope_v[:, :, bass.ds(g * HPG, HPG + 1)]).then_inc(gslope_done, 1)
                dve.wait_ge(gslope_done, it + (1 + C))

                def head_out(j):
                    dve.wait_ge(unit_used, it * G_UNITS + ((j + 1) * H_UNITS + C))
                    dve.wait_ge(o_norm, it * HPG + (j + C))
                    nc.vector.tensor_reduce(ored[:, :, :], ops[:, :].rearrange("p (i c d) -> p i d c", i=TT, c=2),
                                            AX.X, ALU.add).then_inc(o_read, 1)
                    nc.vector.reciprocal(rsum[:, :], sums[:, j % 2, :]).then_inc(rsum_done, 1)

                def first_read(n, kind, i):
                    half = th[:, i % 2 * FW:(i % 2 + 1) * FW]
                    if kind == "ffn":
                        dve.wait_ge(th_done, gth + (tanhs("ffn", i) + C))
                        nc.vector.scalar_tensor_tensor(out=half, in0=half, scalar=1.0, in1=work[BANK[n]][:, 0:FW],
                                                       op0=ALU.add, op1=ALU.mult).then_inc(ga_done, 1)
                    elif kind == "y":
                        dve.wait_ge(ss_done, it * SUBS + (i + 1 + C))
                        y_unit = 1.0 / (H_SCALE * F_SCALE)
                        c = (0.5 * y_unit) ** -2
                        q = i % SUBS
                        nc.vector.tensor_scalar(rbase[:, q:q + 1], ssq[:, q:q + 1], y_unit ** 2 / D * c,
                                                RMS_EPS * c, ALU.mult, ALU.add).then_inc(rb_done, 1)
                    else:
                        dve.wait_ge(qk_f32, it * 4 + (i + 5 + C))
                        dve.sem_inc(work_free, 1)

                def second_read(n, kind, i):
                    if kind == "ffn":
                        half = th[:, i % 2 * FW:(i % 2 + 1) * FW]
                        dve.wait_ge(ga_done, it * FT + (i + 1 + C))
                        nc.vector.scalar_tensor_tensor(
                            out=half, in0=half, scalar=0.5 * H_SCALE / (X_SCALE * F_SCALE) ** 2,
                            in1=work[BANK[n]][:, FW:2 * FW], op0=ALU.mult, op1=ALU.mult).then_inc(work_free, 1)

                def last_read(n, kind, i):
                    if kind == "y":
                        dve.wait_ge(th_done, gth + (tanhs("y", i) + C))
                        nc.vector.scalar_tensor_tensor(out=th[:, :], in0=th[:, :], scalar=1.0, in1=work[BANK[n]][:, :],
                                                       op0=ALU.add, op1=ALU.mult).then_inc(work_free, 1)
                        dve.wait_ge(work_free, gw + (n + 1 + C))
                        dve.wait_ge(g_out, it * (SUBS * 16) + (i * 16 + 16))
                        nc.vector.tensor_scalar(gst[:, :], th[:, :], rr[:, i % SUBS:i % SUBS + 1], None,
                                                ALU.mult).then_inc(g_done, 1)
                    elif kind == "qk":
                        qk_to_lo(it + 1, i)

                for s in range(STEPS if more else STEPS + 2):
                    fill = fill_of(prev, more, s)
                    ahead = s + 1 < STEPS + more
                    if ahead:
                        masked_max(gs, gu, s + 1)
                    if fill:
                        first_read(*fill)
                    if fill:
                        second_read(*fill)
                    if (prev or s >= 1) and s <= STEPS:
                        for n, u in enumerate(units_of(s - 1)):
                            w = min(4, TILE[(s - 1) % TT] + 1 - 4 * n) * P
                            unit_to_lo(gu, u, pt_sb[:, u % 4, 1, 0:w], pt_sb[:, u % 4, 0, 0:w], w, 0)
                    if fill:
                        last_read(*fill)
                    if s > TT and s % TT == 1 or prev and s == 1:
                        head_out(s // TT - 1)

                def last_gates():
                    first_read(*ENDED[False][STEPS + 2])
                    last_read(*ENDED[False][STEPS + 2])

                return last_gates

            def token_stats(b, t):
                nc.vector.bn_stats(stats[:, t, :], x_buf[:, t, :]).then_inc(bn_done, 1)

            def token_base(b):
                bt = dve.snap(b * TT)
                for t in range(TT):
                    hold(dve, "dve", bn_done, bt + (t + 1 + C))
                    nc.vector.bn_aggr(mv[:, t, :], stats[:, t, :]).then_inc(mv_done, 1)
                dve.wait_ge(mv_done, bt + (TT + C))
                nc.vector.tensor_scalar(base[:, :], mv[:, :, 1], X_SCALE ** -2, LN_EPS * X_SCALE ** -2,
                                        ALU.mult, ALU.add).then_inc(base_done, 1)

            def normalise(b, t):
                if t == 0:
                    dve.wait_ge(rstd_done, b + (1 + C))
                nc.vector.tensor_scalar(x_buf[:, t, :], x_buf[:, t, :], mv[:, t, 0:1], rstd[:, t:t + 1],
                                        ALU.subtract, ALU.mult).then_inc(xn_done, 1)

            def prepare(b, beside=None):
                un = dve.snap(b * UB)
                sl = dve.snap(b * SB)
                r = 0
                for kind, i in FIRST_ROW if beside else NEXT_ROWS:
                    if kind == "x":
                        unit_to_lo(un, i, xT[:, 1, :, i * P:(i + 1) * P], xT[:, 0, :, i * P:(i + 1) * P], KT * P, KT)
                        continue
                    if kind == "qk":
                        dve.wait_ge(qk_f32, b * GROUPS * 4 + (i + 1 + C))
                        dve.sem_inc(slot_free, 1)
                        qk_to_lo(b * GROUPS, i)
                    else:
                        dve.wait_ge(v_hi, b * TT + (i + 1 + C))
                        nc.vector.scalar_tensor_tensor(
                            out=vals_v[:, i, :, 1, :], in0=three[r % 3].rearrange("p (h d) -> p h d", h=HEADS),
                            scalar=V_SCALE / (X_SCALE * W_SCALE), in1=vals_v[:, i, :, 0, :],
                            op0=ALU.mult, op1=ALU.subtract).then_inc(slot_free, 1)
                    if beside:
                        beside(r)
                    r += 1
                if beside:
                    beside(PRE_SLOTS)
                masked_max(sl + PRE_SLOTS, un + TT, 0)

            def row(b, last):
                un = dve.snap(b * UB)
                sl = dve.snap(b * SB)
                bt = dve.snap(b * TT)
                group(b, 0, False, True)
                with dve.Fori(1, GROUPS - 1) as g:
                    group(b, g, True, True)
                last_gates = group(b, GROUPS - 1, True, False)

                def combine(m):
                    dve.wait_ge(slot_full, sl + (PRE_SLOTS + GROUPS * STEPS + m + 1 + C))
                    nc.vector.scalar_tensor_tensor(out=xo[:, m, :], in0=three[m % 3],
                                                   scalar=1.0 / (V_SCALE * W_SCALE), in1=bo_sb[:, :],
                                                   op0=ALU.mult, op1=ALU.add).then_inc(slot_free, 1)

                for n in range(TT):
                    unit_to_lo(un, TT + GROUPS * G_UNITS + n, pt_sb[:, n % 4, 1, :], pt_sb[:, n % 4, 0, :], 512, 0)
                    if n == 1:
                        last_gates()
                    if not last:
                        if n == 1:
                            dve.wait_ge(x_in, b * 16 + 32)
                        for t in range(max(n - 1, 0) * 3, min(n * 3, TT)):
                            token_stats(b + 1, t)
                        if n == TT // 2:
                            token_base(b + 1)
                    if n >= 1:
                        combine(n - 1)
                    if not last and n > TT // 2:
                        for t in range((n - 5) * TT // 3, (n - 4) * TT // 3):
                            normalise(b + 1, t)
                combine(TT - 1)
                if not last:
                    prepare(b + 1)

            def decode(k):
                words, _, no, ng, _ = batches[k]
                nw = no * ng * 16
                m = mags[k % 2]
                if k >= 1:
                    dve.wait_ge(codes, k)
                if k >= 2:
                    dve.wait_ge(wf_done, 4 * (k - 1))
                for q in range(4):
                    for dst, bit, mask in ((m, 9 - 4 * q, 0x0E000E00), (signs, 12 - 4 * q, 0x80008000)):
                        op = ALU.logical_shift_left if bit >= 0 else ALU.logical_shift_right
                        nc.vector.tensor_scalar(dst[:, q, 0:nw].rearrange("p (t w) -> p t w", t=no), words,
                                                abs(bit), mask, op, ALU.bitwise_and).then_inc(bits, 1)
                dve.wait_ge(bits, 8 * (k + 1))
                nc.vector.tensor_tensor(m[:, :, 0:nw], m[:, :, 0:nw], signs[:, :, 0:nw],
                                        ALU.bitwise_or).then_inc(codes, 1)

            def batch_to_lo(k):
                _, _, no, ng, dst = batches[k]
                for g in range(ng):
                    n = first_of[k] + g
                    dve.wait_ge(bank_hi, n + 1)
                    nc.vector.tensor_tensor(dst[g][1], banks[n % 5][:, 0:no * P], dst[g][0],
                                            ALU.subtract).then_inc(bank_lo, 1)

            def split(n, source, hi, lo):
                dve.wait_ge(split_hi, n + 1)
                nc.vector.scalar_tensor_tensor(out=lo, in0=source, scalar=W_SCALE, in1=hi, op0=ALU.mult,
                                               op1=ALU.subtract).then_inc(split_lo, 1)

            nc.vector.memset(neghalf[:, :], -0.5)
            unit = F_SCALE * 2.0 ** 14
            dve.wait_ge(scales_t, 1)
            nc.vector.tensor_scalar(scl[:, 0:GU_T * KT], work[0][:, :].bitcast(F16)[:, 0:GU_T * KT], unit, None,
                                    ALU.mult).then_inc(scl_done, 1)
            pd = work[1][:, :].bitcast(F16)[:, 0:DN_T * 16].rearrange("p (t g) -> p t g", t=DN_T)
            s0, parts = GU_T * KT, 1
            for g0 in range(0, FT, 4):
                ng = min(4, FT - g0)
                nc.vector.tensor_scalar(scl[:, s0:s0 + DN_T * ng].rearrange("p (t g) -> p t g", t=DN_T),
                                        pd[:, :, g0:g0 + ng], unit, None, ALU.mult).then_inc(scl_done, 1)
                s0 += DN_T * ng
                parts += 1
            dve.wait_ge(scl_done, parts)
            dve.wait_ge(gu_loaded, 16)
            decode(0)
            decode(1)
            dve.wait_ge(x_in, 16)
            for t in range(TT):
                token_stats(0, t)
            token_base(0)
            batch_to_lo(0)
            for t in range(TT):
                normalise(0, t)
            for k in range(KT):
                split(k, wqkv_in[k], wqkv_sb[:, 0, k, :], wqkv_sb[:, 1, k, :])
            split(KT, wo_in, wo_sb[:, 0, :, :], wo_sb[:, 1, :, :])
            dve.wait_ge(small_in, 16 * 5)
            nc.vector.tensor_tensor(colb[:, :], colb[:, :], col[:, 8:16], ALU.mult).then_inc(bias_done, 1)
            rows = bv_in.unsqueeze(2).broadcast_to([P, KT, P])
            nc.vector.tensor_scalar(bv_rows[:, 0, :, :], rows, V_SCALE, None, ALU.mult).then_inc(bv_done, 1)
            dve.wait_ge(bv_done, 1)
            nc.vector.scalar_tensor_tensor(out=bv_rows[:, 1, :, :], in0=rows, scalar=V_SCALE, in1=bv_rows[:, 0, :, :],
                                           op0=ALU.mult, op1=ALU.subtract).then_inc(bv_done, 1)
            decode(2)
            dve.wait_ge(dn_loaded, 16)

            def beside(r):
                decoding_beside(r, decode, batch_to_lo)
                if r == PRE_SLOTS:
                    dve.wait_ge(bv_wo, 1)
                    nc.vector.scalar_tensor_tensor(out=bo_sb[:, :], in0=ops[:, :], scalar=1.0 / (V_SCALE * W_SCALE),
                                                   in1=bo_sb[:, :], op0=ALU.mult, op1=ALU.add).then_inc(bias_done, 1)
                    dve.wait_ge(dist_in, 16)

            prepare(0, beside)
            with dve.Fori(0, B - 1) as b:
                row(b, False)
            row(B - 1, True)


_INS = ["L0_attn_x", "L0_attn_Wqkv", "L0_attn_bqkv", "L0_attn_Wo", "L0_attn_bo", "L0_ffn_gate_up_packed",
        "L0_ffn_gate_up_scales", "L0_ffn_down_packed", "L0_ffn_down_scales"]


def kernel(**inputs):
    import concourse.bacc as bacc
    from concourse.bass_utils import run_bass_kernel_spmd

    nc = bacc.Bacc("TRN2", target_bir_lowering=False, num_devices=1)
    arrays = {name: np.ascontiguousarray(inputs[name]) for name in _INS}
    arrays |= {f"const_{k}": v for k, v in shape_constants(arrays["L0_attn_x"].shape[1]).items()}
    args = [nc.dram_tensor(f"in_{k}", a.shape, mybir.dt.from_np(a.dtype), kind="ExternalInput").ap()
            for k, a in arrays.items()]
    out = nc.dram_tensor("out_0", arrays["L0_attn_x"].shape, F32, kind="ExternalOutput").ap()
    gates = nc.dram_tensor("gates", [out.shape[0] * out.shape[1], out.shape[2]], F32, kind="Internal").ap()
    gated_attention_ffn(nc, *args, gates, out)
    r = run_bass_kernel_spmd(nc, [{f"in_{k}": a for k, a in arrays.items()}], core_ids=[0])
    return r.results[0]["out_0"]
```
